# Optimizing a Trainium2 kernel written in Bass

```python
import numpy as np
import jax
import jax.numpy as jnp

def _softmax(x, axis=-1):
    return jax.nn.softmax(x, axis=axis)

def _gelu(x):
    return jax.nn.gelu(x, approximate=True)

def _silu(x):
    return jax.nn.silu(x)

def _sigmoid(x):
    return jax.nn.sigmoid(x)

def _layernorm(x, axis=-1, eps=1e-05):
    m = jnp.mean(x, axis=axis, keepdims=True)
    v = jnp.var(x, axis=axis, keepdims=True)
    return (x - m) / jnp.sqrt(v + eps)

def _scatter_add(tgt, idx, src, axis=0):
    return tgt.at[idx].add(src)

def _segment_sum(src, seg, n):
    return jax.ops.segment_sum(src, seg, n)
kernel_name = 'mk_flamingo_gated_d1_seqx_r4_bbd7c3'

def setup_inputs(seed: int=0):
    np.random.seed(seed)
    _w = jnp.asarray

    def _rec_inputs():
        import jax
        import jax.numpy as jnp
        _rk = jax.random.key(seed)
        x = 7.22e-05 + 1 * jax.random.normal(jax.random.fold_in(_rk, 1), (8, 256, 256), jnp.float32)
        _lenS = 256 - jax.random.randint(jax.random.fold_in(_rk, 7), (8,), 0, max(1, 256 // 4) + 1, jnp.int32)
        _lenS2 = 120 - jax.random.randint(jax.random.fold_in(_rk, 8), (8,), 0, max(1, 120 // 4) + 1, jnp.int32)
        _ctx_1024P = jax.random.normal(jax.random.fold_in(_rk, 11), (8, 16, 256), jnp.float32)
        _ctx_1024c = jax.random.dirichlet(jax.random.fold_in(_rk, 511), 0.3 * jnp.ones((16,), jnp.float32), (8, 120))
        _ctx_1024t = jnp.einsum('bsk,bkd->bsd', _ctx_1024c, _ctx_1024P)
        _ctx_1024t = _ctx_1024t * jax.lax.rsqrt(jnp.mean(jnp.square(_ctx_1024t)) + 1e-12) * 0.953939
        ctx_1024 = -1.52775e-05 + 0.999936 * (_ctx_1024t + 0.3 * jax.random.normal(jax.random.fold_in(_rk, 611), (8, 120, 256), jnp.float32))
        _g = jax.random.normal(jax.random.fold_in(_rk, 9001), (2, 1), jnp.float32)
        _g = jnp.sign(_g) * jnp.maximum(jnp.abs(_g), 1.0) + (_g == 0) * 1.0
        g_xattn = _g[0]
        g_ffn = _g[1]
        return (x, ctx_1024, g_xattn, g_ffn)
    x, ctx_1024, g_xattn, g_ffn = _rec_inputs()

    def _L0_xattn_setup():
        import jax, jax.numpy as jnp
        import numpy as np
        HIDDEN = 256
        key = jax.random.key(seed)
        ks = jax.random.split(key, 8)
        s = 1.0 / np.sqrt(HIDDEN)
        return {'query': jax.random.normal(ks[0], (8, 256, HIDDEN), dtype=jnp.float32), 'ref': jax.random.normal(ks[1], (8, 1024, HIDDEN), dtype=jnp.float32), 'Wq': jax.random.normal(ks[2], (HIDDEN, HIDDEN), dtype=jnp.float32) * s, 'bq': jax.random.normal(ks[3], (HIDDEN,), dtype=jnp.float32) * s, 'Wk': jax.random.normal(ks[4], (HIDDEN, HIDDEN), dtype=jnp.float32) * s, 'bk': jax.random.normal(ks[5], (HIDDEN,), dtype=jnp.float32) * s, 'Wv': jax.random.normal(ks[6], (HIDDEN, HIDDEN), dtype=jnp.float32) * s, 'bv': jax.random.normal(ks[7], (HIDDEN,), dtype=jnp.float32) * s}
    _L0_xattn_all = _L0_xattn_setup()
    _L0_xattn_in = {k: v for k, v in _L0_xattn_all.items() if k in ('Wq', 'bq', 'Wk', 'bk', 'Wv', 'bv')}
    del _L0_xattn_all

    def _L0_ffn_setup():
        import jax, jax.numpy as jnp
        import numpy as np
        S, B, H, I, E = (128, 2, 256, 704, 8)
        key = jax.random.key(seed)
        ks = jax.random.split(key, 5)
        return {'hidden_states': jax.random.normal(ks[0], (S, B, H), dtype=jnp.float32), 'router_w': jax.random.normal(ks[1], (E, H), dtype=jnp.float32) * 0.02, 'gate_w': jax.random.normal(ks[2], (E, I, H), dtype=jnp.float32) * 0.02, 'up_w': jax.random.normal(ks[3], (E, I, H), dtype=jnp.float32) * 0.02, 'down_w': jax.random.normal(ks[4], (E, H, I), dtype=jnp.float32) * 0.02}
    _L0_ffn_all = _L0_ffn_setup()
    _L0_ffn_in = {k: v for k, v in _L0_ffn_all.items() if k in ('router_w', 'gate_w', 'up_w', 'down_w')}
    del _L0_ffn_all
    return {'x': x, 'ctx_1024': ctx_1024, 'g_xattn': g_xattn, 'g_ffn': g_ffn, 'L0_xattn_Wq': _L0_xattn_in['Wq'], 'L0_xattn_bq': _L0_xattn_in['bq'], 'L0_xattn_Wk': _L0_xattn_in['Wk'], 'L0_xattn_bk': _L0_xattn_in['bk'], 'L0_xattn_Wv': _L0_xattn_in['Wv'], 'L0_xattn_bv': _L0_xattn_in['bv'], 'L0_ffn_router_w': _L0_ffn_in['router_w'], 'L0_ffn_gate_w': _L0_ffn_in['gate_w'], 'L0_ffn_up_w': _L0_ffn_in['up_w'], 'L0_ffn_down_w': _L0_ffn_in['down_w']}

def reference(x, ctx_1024, g_xattn, g_ffn, L0_xattn_Wq, L0_xattn_bq, L0_xattn_Wk, L0_xattn_bk, L0_xattn_Wv, L0_xattn_bv, L0_ffn_router_w, L0_ffn_gate_w, L0_ffn_up_w, L0_ffn_down_w):
    import jax
    import jax.numpy as jnp

    def _L0_xattn_ref(query, ref, Wq, bq, Wk, bk, Wv, bv):
        import jax, jax.numpy as jnp
        import numpy as np
        HIDDEN = 256
        norm_fact = 1.0 / np.sqrt(HIDDEN).astype(np.float32)
        Q = query @ Wq + bq
        K = ref @ Wk + bk
        V = ref @ Wv + bv
        scores = jnp.einsum('bqh,bkh->bqk', Q, K)
        attn = jax.nn.softmax(scores, axis=-1) * norm_fact
        return jnp.einsum('bqk,bkh->bqh', attn, V)

    def _L0_ffn_ref(hidden_states, router_w, gate_w, up_w, down_w):
        import jax, jax.numpy as jnp
        import numpy as np
        S, B, H, I, E = (128, 2, 256, 704, 8)
        router_logits = jnp.einsum('sbh,eh->sbe', hidden_states, router_w)
        routing_indices = jnp.argmax(router_logits, axis=-1)
        out = jnp.zeros_like(hidden_states)
        for e in range(E):
            mask = (routing_indices == e)[..., None]
            xe = jnp.where(mask, hidden_states, 0.0)
            g = jnp.einsum('sbh,ih->sbi', xe, gate_w[e])
            u = jnp.einsum('sbh,ih->sbi', xe, up_w[e])
            ye = jnp.einsum('sbi,hi->sbh', jax.nn.silu(g) * u, down_w[e])
            out = out + jnp.where(mask, ye, 0.0)
        return out
    x = x + jnp.tanh(g_xattn[0]) * _L0_xattn_ref(_layernorm(x, axis=-1), ctx_1024, L0_xattn_Wq, L0_xattn_bq, L0_xattn_Wk, L0_xattn_bk, L0_xattn_Wv, L0_xattn_bv)
    x = x + jnp.tanh(g_ffn[0]) * _L0_ffn_ref(_layernorm(x, axis=-1), L0_ffn_router_w, L0_ffn_gate_w, L0_ffn_up_w, L0_ffn_down_w)
    return x

_drawn_inputs = setup_inputs


def setup_inputs(seed=0):
    import zlib

    import numpy as np

    out = dict(_drawn_inputs(seed))
    spreads = {}
    factors = {'L0_xattn_bq': 7.236, 'L0_xattn_bk': 8.0, 'L0_xattn_bv': 8.0}
    for name, (base, spread) in spreads.items():
        noise = np.random.default_rng([zlib.crc32(name.encode()), seed]).standard_normal(out[name].shape)
        drawn = base * np.exp(spread * noise) if base else spread * noise
        out[name] = jnp.asarray(drawn.astype(out[name].dtype))
    for name, factor in factors.items():
        out[name] = (out[name] * factor).astype(out[name].dtype)
    return out
```

```python
from contextlib import ExitStack

import concourse.bass as bass
from concourse import mybir

F32 = mybir.dt.float32
BF16 = mybir.dt.bfloat16
I32 = mybir.dt.int32
U32 = mybir.dt.uint32
ALU = mybir.AluOpType
ACT = mybir.ActivationFunctionType
AX_X = mybir.AxisListType.X

P = 128
B, S, H = 8, 256, 256
K = 120
N = B * S
E, I = 8, 704
C = H // P
TB = S // P
NTOK = N // P
NT = (N + E - 1 + E * (P - 1)) // P
HALF = I // 2
CI = (I + P - 1) // P
LAST = I - (CI - 1) * P
ROW = H + 2
RING = 4
EPS = 1e-5
MAGIC = 0x5F3759DF
NORM = H ** -0.5


def flamingo_moe(nc, x, ctxT, g_x, g_f, WqT, WkT, Wv, bv, WrT, Wgu, Wd, WdL, out):
    with ExitStack() as stack:
        def sb(name, shape, dt=F32):
            return stack.enter_context(nc.sbuf_tensor(name, shape, dt))

        def sem(name):
            return stack.enter_context(nc.semaphore(name))

        rows = nc.dram_tensor("x1_rows", (N + 1, ROW), F32, kind="Internal").ap()

        wgu = sb("wgu", [P, E, C, 4, HALF])
        wd = sb("wd", [P, E, CI, H])
        ctx_sb = sb("ctx_sb", [P, C, B * K])
        wqT = sb("wqT", [P, C, H + 1])
        wkT = sb("wkT", [P, C, H + 1])
        wv = sb("wv", [P, C, H])
        wrT = sb("wrT", [P, C, E])
        bvb = sb("bvb", [P, H])
        gates = sb("gates", [P, 2])
        tg = sb("tg", [P, 2])
        tgn = sb("tgn", [P, 1])
        ident = sb("ident", [P, P])
        ones_row = sb("ones_row", [1, P])
        tri = sb("tri", [P, P], BF16)
        ones_b = sb("ones_b", [P, P], BF16)
        iota_p = sb("iota_p", [P, 1])
        iota_lo = sb("iota_lo", [P, P])
        iota_hi = sb("iota_hi", [P, NTOK, NT])
        iota_t = sb("iota_t", [P, NTOK, NT])
        iota_e = sb("iota_e", [P, E])
        starts = sb("starts", [P, NT, E])
        zrow = sb("zrow", [1, ROW])
        MT = sb("MT", [P, C, H + 1])
        wqbk = sb("wqbk", [P, C + 1])
        A = sb("A", [P, C, B * K])
        brow = sb("brow", [1, B * K])
        V = sb("V", [K, B, H])
        xin = sb("xin", [P, NTOK, H])
        st1 = sb("st1", [P, NTOK, 6])
        mv1 = sb("mv1", [P, NTOK, 2])
        rs1 = sb("rs1", [P, NTOK])
        nm1 = sb("nm1", [P, NTOK])
        nwt = sb("nwt", [P, 4, NTOK])
        xn = sb("xn", [P, TB, H])
        xnT = sb("xnT", [P, C, S])
        negmax = sb("negmax", [P, TB])
        ssum = sb("ssum", [P, 2, TB])
        prob = sb("prob", [P, TB, K])
        pT = sb("pT", [K, S])
        orow = sb("orow", [P, 2, TB])
        x1 = sb("x1", [P, 2, TB, ROW])
        st2 = sb("st2", [P, TB, 6])
        mv2 = sb("mv2", [P, TB, 2])
        xn2, xn2T = wkT[:, :, 0:H], wv[:]
        top8 = sb("top8", [P, TB, 8])
        idx8 = sb("idx8", [P, TB, 8], U32)
        pick = sb("pick", [P, TB])
        oh = sb("oh", [P, NTOK, E], BF16)
        cum = sb("cum", [P, NTOK + 1, E], BF16)
        cnt = sb("cnt", [P, 5, E])
        cnt_i = sb("cnt_i", [P, 2, E], I32)
        slot = sb("slot", [P, NTOK])
        slot_i = sb("slot_i", [P, 3, NTOK], I32)
        slot_f = sb("slot_f", [P, 2, NTOK])
        tabf = sb("tabf", [P, NT])
        tab2 = sb("tab2", [P, NT])
        table = sb("table", [P, NT], I32)
        exf = sb("exf", [P, NT])
        expert = sb("expert", [P, NT], I32)
        free_x = xin[:].rearrange("p t h -> p (t h)")
        free_a = A[:].rearrange("p c n -> p (c n)")

        def part(room, start, *dims):
            size = 1
            for d in dims:
                size *= d
            names = " ".join("abc"[:len(dims)])
            view = room[:, start:start + size]
            if len(dims) > 1:
                view = view.rearrange(f"p ({names}) -> p {names}", **dict(zip("abc", dims)))
            return view, start + size

        free_c = ctx_sb[:].rearrange("p c n -> p (c n)")
        ohhi, at = part(free_c, 0, NTOK, NT)
        ohlo, _ = part(free_c[:, at:at + NTOK * P // 2].bitcast(BF16), 0, NTOK, P)
        at += NTOK * P // 2
        uv, _ = part(free_c[:, at:at + NTOK * NT].bitcast(BF16), 0, NTOK, 2, NT)

        free_q = wqT[:].rearrange("p c n -> p (c n)")
        past, at = part(free_q, 0, NT, E)
        rk, at = part(free_q, at, NTOK, E)

        xg, at = part(free_x, 0, RING, ROW)
        og, at = part(free_x, at, RING, H)
        xh, at = part(free_x, at, 2, H)
        xhT, at = part(free_x, at, 2, C, P)
        sg, at = part(free_x, at, I)
        hm, at = part(free_a, 0, I)
        hT, at = part(free_a, at, CI, P)

        ps = stack.enter_context(nc.psum_tensor("ps", [P, 8, 512], F32))

        d_x = [sem(f"d_x{i}") for i in range(B)]
        d_wq, d_ctx, d_sm, d_g = sem("d_wq"), sem("d_ctx"), sem("d_sm"), sem("d_g")
        d_w = [sem(f"d_w{e}") for e in range(E)]
        w_ready = sem("w_ready")
        k_pool = sem("k_pool")
        a_tg, v_tg = sem("a_tg"), sem("v_tg")
        t_mt, a_mt = sem("t_mt"), sem("a_mt")
        t_v, v_v = sem("t_v"), sem("v_v")
        t_a, a_a = sem("t_a"), sem("a_a")
        t_br, a_br = sem("t_br"), sem("a_br")
        v_chain = sem("v_chain")
        v_st1 = sem("v_st1")
        a_xn, t_t1, a_xnT = sem("a_xn"), sem("t_t1"), sem("a_xnT")
        t_s, v_max, a_exp = sem("t_s"), sem("v_max"), sem("a_exp")
        t_t2, a_pT, t_pv = sem("t_t2"), sem("a_pT"), sem("t_pv")
        v_x1, d_row = sem("v_x1"), [sem("d_row0"), sem("d_row1")]
        d_zrow = sem("d_zrow")
        a_xn2, t_t3, a_xn2T = sem("a_xn2"), sem("t_t3"), sem("a_xn2T")
        t_lg, v_oh = sem("t_lg"), sem("v_oh")
        t_rk, v_lo, t_tab, v_tab, v_exp = sem("t_rk"), sem("v_lo"), sem("t_tab"), sem("v_tab"), sem("v_exp")
        d_gath = [sem(f"d_gath{r}") for r in range(RING)]
        d_scat = [sem(f"d_scat{r}") for r in range(RING)]
        a_xh, t_tx, a_xhT = sem("a_xh"), sem("t_tx"), sem("a_xhT")
        t_gu, a_sg, v_h = sem("t_gu"), sem("a_sg"), sem("v_h")
        t_th, a_hT, v_hT = sem("t_th"), sem("a_hT"), sem("v_hT")
        t_y, v_out = sem("t_y"), sem("v_out")
        idle = {n: sem(f"idle_{n}") for n in ("pe", "act", "dve", "pool", "sp")}

        def after(eng, name, s, value):
            if isinstance(value, int):
                if value > 0:
                    eng.wait_ge(s, value)
            else:
                eng.wait_ge(s, value)
                eng.sem_inc(idle[name], 1)

        block = stack.enter_context(nc.Block())

        @block.sync
        def _(sp):
            def ap(t, c):
                return t.rearrange("(c p) n -> p c n", c=c)

            sp.dma_start(wkT[:], ap(WkT, C)).then_inc(d_wq, 16)
            sp.dma_start(wqT[:], ap(WqT, C)).then_inc(d_wq, 16)
            sp.dma_start(ctx_sb[:], ap(ctxT, C)).then_inc(d_ctx, 16)
            sp.dma_start(wv[:], ap(Wv, C)).then_inc(d_ctx, 16)
            xv = x.rearrange("b (t p) h -> b p t h", p=P)
            for b in range(B):
                sp.dma_start(xin[:, TB * b:TB * b + TB, :], xv[b]).then_inc(d_x[b], 16)
            for e in range(E):
                sp.dma_start(wgu[:, e].rearrange("p c g n -> p (c g n)"), Wgu[e]).then_inc(d_w[e], 16)
                sp.dma_start(wd[:, e, 0:CI - 1, :].rearrange("p c n -> p (c n)"), Wd[e]).then_inc(d_w[e], 16)
                sp.dma_start(wd[0:LAST, e, CI - 1, :], WdL[e]).then_inc(d_w[e], 16)
            sp.wait_ge(k_pool, 1)
            sp.dma_start(rows[N:N + 1, :], zrow[:]).then_inc(d_zrow, 16)

            rv = rows[0:N].rearrange("(b t p) h -> b p t h", p=P, t=TB)

            def store(i, par):
                after(sp, "sp", v_x1, i + 1)
                sp.dma_start(rv[bass.ds(i, 1)].rearrange("b p t h -> p (b t) h"), x1[:, par]).then_inc(d_row[par], 16)

            store(0, 0)
            store(1, 1)
            with sp.Fori(1, B // 2, 1) as h:
                store(2 * h, 0)
                store(2 * h + 1, 1)
            for e in range(E):
                sp.wait_ge(d_w[e], 48)
                sp.sem_inc(w_ready, 1)

        @block.gpsimd
        def _(pool):
            kinds = [
                lambda: pool.memset(zrow[:], 0.0),
                lambda: pool.memset(ident[:], 0.0),
                lambda: pool.memset(tri[:], 1.0),
                lambda: pool.memset(ones_b[:], 1.0),
                lambda: pool.memset(ones_row[:], 1.0),
                lambda: pool.memset(cum[:, 0, :], 0.0),
            ]
            for make in kinds:
                make().then_inc(k_pool, 1)
            fl = dict(allow_small_or_imprecise_dtypes=True)
            pool.wait_ge(k_pool, 6)
            pool.affine_select(out=ident[:], in_=ident[:], compare_op=ALU.not_equal, fill=1.0, base=0,
                               pattern=[[-1, P]], channel_multiplier=1).then_inc(k_pool, 1)
            pool.affine_select(out=tri[:], in_=tri[:], compare_op=ALU.is_gt, fill=0.0, base=0,
                               pattern=[[1, P]], channel_multiplier=-1).then_inc(k_pool, 1)
            pool.iota(iota_p[:], pattern=[[0, 1]], base=0, channel_multiplier=1, **fl).then_inc(k_pool, 1)
            pool.iota(iota_lo[:], pattern=[[1, P]], base=0, channel_multiplier=0, **fl).then_inc(k_pool, 1)
            pool.iota(iota_e[:], pattern=[[1, E]], base=0, channel_multiplier=0, **fl).then_inc(k_pool, 1)
            pool.iota(iota_hi[:], pattern=[[0, NTOK], [1, NT]], base=0, channel_multiplier=0, **fl).then_inc(k_pool, 1)
            pool.iota(iota_t[:], pattern=[[1, NTOK], [0, NT]], base=-NTOK, channel_multiplier=0, **fl).then_inc(k_pool, 1)
            pool.iota(starts[:], pattern=[[P, NT], [0, E]], base=0, channel_multiplier=0, **fl).then_inc(k_pool, 1)

            for par in range(2):
                pool.wait_ge(d_row[par], 16 * (B // 2))
            pool.wait_ge(d_zrow, 16)
            pool.wait_ge(v_tab, 1)

            idx = table

            def gather(j):
                pool.indirect_dma_start(
                    out=xg[:, j % RING, :], out_offset=None, in_=rows,
                    in_offset=bass.IndirectOffsetOnAxis(ap=idx[:, j:j + 1], axis=0)).then_inc(d_gath[j % RING], 16)

            def scatter(j):
                pool.indirect_dma_start(
                    out=out, out_offset=bass.IndirectOffsetOnAxis(ap=idx[:, j:j + 1], axis=0),
                    in_=og[:, j % RING, :], in_offset=None, bounds_check=N - 1,
                    oob_is_err=False).then_inc(d_scat[j % RING], 16)

            for j in range(RING):
                gather(j)
            for j in range(NT):
                pool.wait_ge(v_out, j + 1)
                if j + RING < NT:
                    gather(j + RING)
                scatter(j)
            for r in range(RING):
                pool.wait_ge(d_scat[r], 16 * len(range(r, NT, RING)))

        @block.scalar
        def _(act):
            act.dma_start(gates[:, 0:1], g_x.to_broadcast([P, 1])).then_inc(d_g, 16)
            act.dma_start(gates[:, 1:2], g_f.to_broadcast([P, 1])).then_inc(d_g, 16)
            act.dma_start(bvb[:], bv.to_broadcast([P, H])).then_inc(d_sm, 16)
            act.dma_start(wrT[:], WrT.rearrange("(c p) n -> p c n", c=C)).then_inc(d_sm, 16)
            act.wait_ge(d_g, 32)
            act.activation(tg[:], gates[:], ACT.Tanh).then_inc(a_tg, 1)
            act.wait_ge(t_mt, 1)
            for m in range(C):
                act.activation(MT[:, m, :], ps[:, 4 + m, 0:H + 1], ACT.Copy).then_inc(a_mt, 1)
            act.activation(wqbk[:, 0:C], ps[:, 4, 300:300 + C], ACT.Copy).then_inc(a_mt, 1)
            act.activation(wqbk[0:1, C:C + 1], ps[0:1, 5, 300:301], ACT.Copy).then_inc(a_mt, 1)
            act.wait_ge(a_mt, C + 2)
            for q in range(4):
                m, n = q // 2, q % 2
                act.wait_ge(t_a, q + 1)
                act.activation(A[:, m, 480 * n:480 * n + 480], ps[:, 4 + q, 0:480], ACT.Identity,
                               bias=wqbk[:, m:m + 1]).then_inc(a_a, 1)
            act.wait_ge(t_br, 1)
            for n in range(2):
                act.activation(brow[:, 480 * n:480 * n + 480], ps[0:1, n, 0:480], ACT.Identity,
                               bias=wqbk[0:1, C:C + 1]).then_inc(a_br, 1)

            def norm1(i):
                after(act, "act", t_t1, i)
                for k in range(TB):
                    t = bass.ds(TB * i + k, 1)
                    ins = act.activation(xn[:, k, :], xin[:, t, :].rearrange("p o h -> p (o h)"), ACT.Identity,
                                         scale=rs1[:, t], bias=nm1[:, t])
                ins.then_inc(a_xn, 1)

            def turned1(i):
                after(act, "act", t_t1, i + 1)
                after(act, "act", t_s, i)
                act.activation(xnT[:].rearrange("p c s -> p (c s)"), ps[:, 0, :], ACT.Copy).then_inc(a_xnT, 1)

            def exps(i, par):
                after(act, "act", v_max, i + 1)
                after(act, "act", t_t2, i)
                for k in range(TB):
                    ins = act.activation(prob[:, k, :], ps[:, 2, K * k:K * k + K], ACT.Exp,
                                         bias=negmax[:, k:k + 1], accum_out=ssum[:, par, k:k + 1])
                ins.then_inc(a_exp, 1)

            def turned2(i):
                after(act, "act", t_t2, i + 1)
                after(act, "act", t_pv, i)
                act.activation(pT[:], ps[0:K, 3, 0:S], ACT.Copy).then_inc(a_pT, 1)

            def norm2(i, par):
                after(act, "act", v_x1, i + 1)
                after(act, "act", t_t3, i)
                for k in range(TB):
                    ins = act.activation(xn2[:, k, :], x1[:, par, k, 0:H], ACT.Identity,
                                         scale=x1[:, par, k, H:H + 1], bias=x1[:, par, k, H + 1:H + 2])
                ins.then_inc(a_xn2, 1)

            def turned3(i):
                after(act, "act", t_t3, i + 1)
                after(act, "act", t_lg, i)
                act.activation(xn2T.rearrange("p c s -> p (c s)"), ps[:, 1, :], ACT.Copy).then_inc(a_xn2T, 1)

            act.wait_ge(v_st1, 1)
            norm1(0)
            turned1(0)
            norm1(1)

            def batch(i, par, first=False, last=False, normed=True):
                exps(i, par)
                if not last:
                    turned1(i + 1)
                if not first:
                    norm2(i - 1, 1 - par)
                turned2(i)
                if not first:
                    turned3(i - 1)
                if normed:
                    norm1(i + 2)

            batch(0, 0, first=True)
            batch(1, 1)
            with act.Fori(1, B // 2 - 1, 1) as h:
                batch(2 * h, 0)
                batch(2 * h + 1, 1)
            batch(B - 2, 0, normed=False)
            batch(B - 1, 1, last=True, normed=False)
            norm2(B - 1, 1)
            turned3(B - 1)

            def gathered(m, q):
                j = 4 * m + 3 + q
                r = (3 + q) % RING
                after(act, "act", d_gath[r], 16 * (m + (3 + q) // RING + 1))
                after(act, "act", t_tx, j - 1)
                act.activation(xh[:, (3 + q) % 2, :], xg[:, r, 0:H], ACT.Identity,
                               scale=xg[:, r, H:H + 1], bias=xg[:, r, H + 1:H + 2]).then_inc(a_xh, 1)

            def turned_x(m, q):
                j = 4 * m + 3 + q
                after(act, "act", t_tx, j + 1)
                after(act, "act", t_gu, 4 * (j - 1))
                act.activation(xhT[:, (3 + q) % 2].rearrange("p c t -> p (c t)"), ps[:, 7, 0:H],
                               ACT.Copy).then_inc(a_xhT, 1)

            def turned_h(m, q):
                j = 4 * m + 3 + q
                after(act, "act", t_th, j + 1)
                after(act, "act", t_y, j)
                act.activation(hT[:, 0:4, :].rearrange("p c t -> p (c t)"), ps[:, 4, :], ACT.Copy).then_inc(a_hT, 1)

            def silus(m, q):
                j = 4 * m + 3 + q
                for half in range(2):
                    after(act, "act", t_gu, 4 * j + 2 * half + 1)
                    after(act, "act", v_h, 2 * (j - 1) + half + 1)
                    act.activation(sg[:, HALF * half:HALF * half + HALF], ps[:, 2 * half, 0:HALF],
                                   ACT.Silu).then_inc(a_sg, 1)

            def tile(m, q, first=False, ahead1=True, ahead2=True):
                if not first:
                    turned_h(m, q - 1)
                if ahead1:
                    turned_x(m, q + 1)
                if ahead2:
                    gathered(m, q + 2)
                silus(m, q)

            gathered(-1, 1)
            turned_x(-1, 1)
            gathered(-1, 2)
            for j in range(3):
                tile(-1, j + 1, first=(j == 0))
            for q in range(4):
                tile(0, q)
            with act.Fori(1, NT // 4 - 1, 1) as m:
                for q in range(4):
                    tile(m, q)
            m = NT // 4 - 1
            for q in range(4):
                tile(m, q, ahead1=(4 * m + 3 + q + 1 < NT), ahead2=(4 * m + 3 + q + 2 < NT))
            turned_h(m, 3)

        @block.tensor
        def _(pe):
            pe.wait_ge(d_wq, 32)
            for m in range(C):
                for c in range(C):
                    pe.matmul(ps[:, 4 + m, 0:H + 1], wkT[:, c, P * m:P * m + P], wqT[:, c, :],
                              start=(c == 0), stop=(c == C - 1))
            for m in range(C):
                for c in range(C):
                    pe.matmul(ps[:, 4, 300 + m:301 + m], wqT[:, c, P * m:P * m + P], wkT[:, c, H:H + 1],
                              start=(c == 0), stop=(c == C - 1))
            for c in range(C):
                last = pe.matmul(ps[0:1, 5, 300:301], wqT[:, c, H:H + 1], wkT[:, c, H:H + 1],
                                 start=(c == 0), stop=(c == C - 1))
            last.then_inc(t_mt, 1)
            pe.wait_ge(d_ctx, 32)
            for b in range(B):
                for c in range(C):
                    last = pe.matmul(ps[0:K, b // 2, H * (b % 2):H * (b % 2) + H], ctx_sb[:, c, K * b:K * b + K],
                                     wv[:, c, :], start=(c == 0), stop=(c == C - 1))
                last.then_inc(t_v, 1)
            pe.wait_ge(a_mt, C + 2)
            for q in range(4):
                m, n = q // 2, q % 2
                for c in range(C):
                    last = pe.matmul(ps[:, 4 + q, 0:480], MT[:, c, P * m:P * m + P], ctx_sb[:, c, 480 * n:480 * n + 480],
                                     start=(c == 0), stop=(c == C - 1))
                last.then_inc(t_a, 1)
            pe.wait_ge(v_v, 4)
            for n in range(2):
                for c in range(C):
                    last = pe.matmul(ps[0:1, n, 0:480], MT[:, c, H:H + 1], ctx_sb[:, c, 480 * n:480 * n + 480],
                                     start=(c == 0), stop=(c == C - 1))
            last.then_inc(t_br, 1)
            pe.wait_ge(k_pool, 14)

            def turn1(i):
                after(pe, "pe", a_xn, i + 1)
                after(pe, "pe", a_xnT, i)
                for k in range(TB):
                    for c in range(C):
                        last = pe.transpose(ps[:, 0, S * c + P * k:S * c + P * k + P],
                                            xn[:, k, P * c:P * c + P], ident[:])
                last.then_inc(t_t1, 1)

            def scores(i):
                after(pe, "pe", a_xnT, i + 1)
                after(pe, "pe", a_exp, i)
                for k in range(TB):
                    for c in range(C):
                        pe.matmul(ps[:, 2, K * k:K * k + K], xnT[:, c, P * k:P * k + P],
                                  A[:, c, bass.ds(K * i, K)], start=(c == 0), stop=False)
                    last = pe.matmul(ps[:, 2, K * k:K * k + K], ones_row[:], brow[:, bass.ds(K * i, K)],
                                     start=False, stop=True)
                last.then_inc(t_s, 1)

            def turn2(i):
                after(pe, "pe", a_exp, i + 1)
                after(pe, "pe", a_pT, i)
                for k in range(TB):
                    last = pe.transpose(ps[0:K, 3, P * k:P * k + P], prob[:, k, :], ident[:])
                last.then_inc(t_t2, 1)

            def values(i):
                after(pe, "pe", a_pT, i + 1)
                after(pe, "pe", v_x1, i)
                for k in range(TB):
                    last = pe.matmul(ps[:, 6, H * k:H * k + H], pT[:, P * k:P * k + P],
                                     V[:, bass.ds(i, 1), :].rearrange("p o h -> p (o h)"), start=True, stop=True)
                last.then_inc(t_pv, 1)

            def turn3(i):
                after(pe, "pe", a_xn2, i + 1)
                after(pe, "pe", a_xn2T, i)
                for k in range(TB):
                    for c in range(C):
                        last = pe.transpose(ps[:, 1, S * c + P * k:S * c + P * k + P],
                                            xn2[:, k, P * c:P * c + P], ident[:])
                last.then_inc(t_t3, 1)

            def logits(i):
                after(pe, "pe", a_xn2T, i + 1)
                after(pe, "pe", v_oh, i)
                for k in range(TB):
                    for c in range(C):
                        last = pe.matmul(ps[:, 7, E * k:E * k + E], xn2T[:, c, P * k:P * k + P], wrT[:, c, :],
                                         start=(c == 0), stop=(c == C - 1))
                last.then_inc(t_lg, 1)

            def batch(i, first=False, last=False):
                scores(i)
                if not last:
                    turn1(i + 1)
                turn2(i)
                if not first:
                    turn3(i - 1)
                values(i)
                if not first:
                    logits(i - 1)

            pe.wait_ge(v_v, B)
            pe.wait_ge(a_a, 4)
            pe.wait_ge(a_br, 2)
            pe.wait_ge(d_sm, 32)
            turn1(0)
            batch(0, first=True)
            batch(1)
            with pe.Fori(1, B // 2 - 1, 1) as h:
                batch(2 * h)
                batch(2 * h + 1)
            batch(B - 2)
            batch(B - 1, last=True)
            turn3(B - 1)
            logits(B - 1)

            pe.wait_ge(v_oh, B)
            flat = "p t e -> p (t e)"
            pe.matmul(ps[:, 0, 0:NTOK * E], tri[:], oh[:].rearrange(flat), start=True, stop=False)
            pe.matmul(ps[:, 0, 0:NTOK * E], ones_b[:], cum[:, 0:NTOK].rearrange(flat), start=False, stop=True)
            pe.matmul(ps[:, 1, 0:E], ones_b[:], cum[:, NTOK, :], start=True, stop=True).then_inc(t_rk, 1)
            pe.wait_ge(v_lo, 1)
            for t in range(NTOK):
                last = pe.matmul(ps[:, 2, 0:2 * NT], ohlo[:, t, :], uv[:, t].rearrange("p a n -> p (a n)"),
                                 start=(t == 0), stop=(t == NTOK - 1))
            last.then_inc(t_tab, 1)

            pe.wait_ge(v_exp, 1)

            def turn_x(m, q):
                j = 4 * m + 3 + q
                after(pe, "pe", a_xh, j + 1)
                after(pe, "pe", a_xhT, j)
                for c in range(C):
                    last = pe.transpose(ps[:, 7, P * c:P * c + P], xh[:, (3 + q) % 2, P * c:P * c + P], ident[:])
                last.then_inc(t_tx, 1)

            def turn_h(m, q):
                j = 4 * m + 3 + q
                after(pe, "pe", v_h, 2 * (j + 1))
                after(pe, "pe", a_hT, j)
                after(pe, "pe", v_hT, j)
                for c in range(CI):
                    rows_ = P if c < CI - 1 else LAST
                    last = pe.transpose(ps[0:rows_, 4 + c // 4, P * (c % 4):P * (c % 4) + P],
                                        hm[:, P * c:P * c + rows_], ident[:])
                last.then_inc(t_th, 1)

            def up(m, q):
                j = 4 * m + 3 + q
                e = pe.value_load(expert[0:1, bass.ds(j, 1)], min_val=0, max_val=E - 1)
                after(pe, "pe", w_ready, e + 1)
                after(pe, "pe", a_xhT, j + 1)
                for g in range(4):
                    for c in range(C):
                        last = pe.matmul(ps[:, g, 0:HALF], xhT[:, (3 + q) % 2, c, :],
                                         wgu[:, bass.ds(e, 1), c, g, :].rearrange("p o n -> p (o n)"),
                                         start=(c == 0), stop=(c == C - 1))
                    last.then_inc(t_gu, 1)

            def down(m, q):
                j = 4 * m + 3 + q
                e = pe.value_load(expert[0:1, bass.ds(j, 1)], min_val=0, max_val=E - 1)
                after(pe, "pe", a_hT, j + 1)
                after(pe, "pe", v_hT, j + 1)
                after(pe, "pe", v_out, j)
                for c in range(CI):
                    rows_ = P if c < CI - 1 else LAST
                    last = pe.matmul(ps[:, 6, 0:H], hT[0:rows_, c, :],
                                     wd[0:rows_, bass.ds(e, 1), c, :].rearrange("p o n -> p (o n)"),
                                     start=(c == 0), stop=(c == CI - 1))
                last.then_inc(t_y, 1)

            def tile(m, q, first=False, ahead=True):
                if not first:
                    turn_h(m, q - 1)
                if ahead:
                    turn_x(m, q + 1)
                up(m, q)
                if not first:
                    down(m, q - 1)

            turn_x(-1, 1)
            for j in range(3):
                tile(-1, j + 1, first=(j == 0))
            for q in range(4):
                tile(0, q)
            with pe.Fori(1, NT // 4 - 1, 1) as m:
                for q in range(4):
                    tile(m, q)
            m = NT // 4 - 1
            for q in range(4):
                tile(m, q, ahead=(4 * m + 3 + q + 1 < NT))
            turn_h(m, 3)
            down(m, 3)

        @block.vector
        def _(dve):
            chained = [0]

            def link(ins):
                chained[0] += 1
                ins.then_inc(v_chain, 1)
                dve.wait_ge(v_chain, chained[0])

            def newton(chain, var, mean, rs, nm, n):
                ve, y, a = nwt[:, 0, 0:n], nwt[:, 1, 0:n], nwt[:, 2, 0:n]
                chain(dve.tensor_scalar(ve, var, EPS, None, ALU.add))
                chain(dve.tensor_scalar(nwt[:, 3, 0:n].bitcast(I32), ve.bitcast(I32), 1, None, ALU.logical_shift_right))
                chain(dve.tensor_scalar(y.bitcast(I32), nwt[:, 3, 0:n].bitcast(I32), -1.0, float(MAGIC), ALU.mult, ALU.add))
                for step in range(3):
                    chain(dve.tensor_tensor(a, y, y, ALU.mult))
                    chain(dve.tensor_tensor(a, a, ve, ALU.mult))
                    chain(dve.tensor_scalar(a, a, -0.5, 1.5, ALU.mult, ALU.add))
                    chain(dve.tensor_tensor(rs if step == 2 else y, a, y, ALU.mult))
                return dve.scalar_tensor_tensor(out=nm, in0=mean, scalar=-1.0, in1=rs, op0=ALU.mult, op1=ALU.mult)

            dve.wait_ge(a_tg, 1)
            dve.tensor_scalar(tgn[:], tg[:, 0:1], NORM, None, ALU.mult).then_inc(v_tg, 1)
            for b in range(B):
                dve.wait_ge(d_x[b], 16)
                for k in range(TB):
                    ins = dve.bn_stats(st1[:, TB * b + k, :], xin[:, TB * b + k, :])
            link(ins)
            for t in range(NTOK):
                ins = dve.bn_aggr(mv1[:, t, :], st1[:, t, :])
            link(ins)
            newton(link, mv1[:, :, 1], mv1[:, :, 0], rs1[:], nm1[:], NTOK).then_inc(v_st1, 1)
            dve.wait_ge(d_sm, 32)
            for b in range(B):
                dve.wait_ge(t_v, b + 1 + (b + 1) % 2)
                dve.tensor_tensor(V[:, b, :], ps[0:K, b // 2, H * (b % 2):H * (b % 2) + H], bvb[0:K, :],
                                  ALU.add).then_inc(v_v, 1)

            per_batch = [None]

            def chain_of(i, base, length):
                n = [0]

                def chain(ins):
                    n[0] += 1
                    ins.then_inc(v_chain, 1)
                    after(dve, "dve", v_chain, base + length * i + n[0])
                return chain, n

            LINKS_M, LINKS_X, LINKS_R = 1, 3 + 15, 6
            LEN = LINKS_M + LINKS_X + LINKS_R
            base = chained[0]

            def maxima(i):
                chain, n = chain_of(i, base, LEN)
                after(dve, "dve", t_s, i + 1)
                chain(dve.tensor_reduce(nwt[:, 3, 0:TB], ps[:, 2, 0:TB * K].rearrange("p (t k) -> p t k", k=K), AX_X, ALU.max))
                after(dve, "dve", a_exp, i)
                dve.tensor_scalar(negmax[:], nwt[:, 3, 0:TB], -1.0, None, ALU.mult).then_inc(v_max, 1)
                assert n[0] == LINKS_M

            return_ = None

            def residual(i, par, off):
                n = [0]

                def chain(ins):
                    n[0] += 1
                    ins.then_inc(v_chain, 1)
                    after(dve, "dve", v_chain, off + n[0])
                after(dve, "dve", a_exp, i + 1)
                chain(dve.reciprocal(orow[:, 0, :], ssum[:, par, :]))
                chain(dve.tensor_scalar(orow[:, 1, :], orow[:, 0, :], tgn[:, 0:1], None, ALU.mult))
                after(dve, "dve", t_pv, i + 1)
                after(dve, "dve", d_row[par], 8 * (i - par))
                for k in range(TB):
                    t = bass.ds(TB * i + k, 1)
                    ins = dve.scalar_tensor_tensor(
                        out=x1[:, par, k, 0:H], in0=ps[:, 6, H * k:H * k + H], scalar=orow[:, 1, k:k + 1],
                        in1=xin[:, t, :].rearrange("p o h -> p (o h)"), op0=ALU.mult, op1=ALU.add)
                chain(ins)
                for k in range(TB):
                    ins = dve.bn_stats(st2[:, k, :], x1[:, par, k, 0:H])
                chain(ins)
                for k in range(TB):
                    ins = dve.bn_aggr(mv2[:, k, :], st2[:, k, :])
                chain(ins)
                newton(chain, mv2[:, :, 1], mv2[:, :, 0], x1[:, par, :, H], x1[:, par, :, H + 1], TB).then_inc(v_x1, 1)
                return n[0]

            def route(i, off):
                n = [0]

                def chain(ins):
                    n[0] += 1
                    ins.then_inc(v_chain, 1)
                    after(dve, "dve", v_chain, off + n[0])
                after(dve, "dve", t_lg, i + 1)
                for k in range(TB):
                    ins = dve.max(top8[:, k, :], ps[:, 7, E * k:E * k + E])
                chain(ins)
                for k in range(TB):
                    ins = dve.max_index(idx8[:, k, :], top8[:, k, :], ps[:, 7, E * k:E * k + E])
                chain(ins)
                chain(dve.tensor_copy(pick[:], idx8[:, :, 0]))
                for k in range(TB):
                    ins = dve.tensor_scalar(oh[:, bass.ds(TB * i + k, 1), :].rearrange("p o e -> p (o e)"), iota_e[:],
                                            pick[:, k:k + 1], None, ALU.is_equal)
                chain(ins)
                for k in range(TB):
                    ins = dve.tensor_tensor(cum[:, bass.ds(TB * i + k + 1, 1), :], cum[:, bass.ds(TB * i + k, 1), :],
                                            oh[:, bass.ds(TB * i + k, 1), :], ALU.add)
                    if k < TB - 1:
                        chain(ins)
                ins.then_inc(v_oh, 1)
                return n[0]

            LX = 2 + 3 + 2 + 1 + 3 * 4
            LR = 4 + TB - 1
            LEN = 1 + LX + LR

            def batch(i, par, first=False):
                start = base + LEN * i - LX - LR
                n = [0]
                after(dve, "dve", t_s, i + 1)
                dve.tensor_reduce(nwt[:, 3, NTOK - TB:NTOK], ps[:, 2, 0:TB * K].rearrange("p (t k) -> p t k", k=K),
                                  AX_X, ALU.max).then_inc(v_chain, 1)
                if first:
                    start = base
                after(dve, "dve", v_chain, start + 1)
                after(dve, "dve", a_exp, i)
                dve.tensor_scalar(negmax[:], nwt[:, 3, NTOK - TB:NTOK], -1.0, None, ALU.mult).then_inc(v_max, 1)
                if not first:
                    assert residual(i - 1, 1 - par, start + 1) == LX
                    assert route(i - 1, start + 1 + LX) == LR

            dve.wait_ge(k_pool, 14)
            batch(0, 0, first=True)
            batch(1, 1)
            with dve.Fori(1, B // 2, 1) as h:
                batch(2 * h, 0)
                batch(2 * h + 1, 1)
            done = base + LEN * (B - 1) + 1
            residual(B - 1, 1, done)
            route(B - 1, done + LX)
            chained[0] = done + LX + LR

            dve.wait_ge(t_rk, 1)
            n_of, padded, ends, offs = cnt[:, 0, :], cnt[:, 1, :], cnt[:, 2, :], cnt[:, 3, :]
            link(dve.tensor_scalar(n_of, ps[:, 1, 0:E], 1.0, float(P - 1), ALU.max, ALU.add))
            link(dve.tensor_copy(cnt_i[:, 0, :], n_of))
            link(dve.tensor_scalar(cnt_i[:, 1, :], cnt_i[:, 0, :], 7, 7, ALU.logical_shift_right, ALU.logical_shift_left))
            link(dve.tensor_copy(padded, cnt_i[:, 1, :]))
            link(dve.memset(cnt[:, 4, :], 0.0))
            link(dve.tensor_tensor_scan(ends, padded, cnt[:, 4, :], 0.0, ALU.add, ALU.add))
            link(dve.tensor_tensor(offs, ends, padded, ALU.subtract))
            link(dve.tensor_tensor(rk[:], ps[:, 0, 0:NTOK * E].rearrange("p (t e) -> p t e", e=E),
                                   cnt[:, 3:4, :].to_broadcast([P, NTOK, E]), ALU.add))
            link(dve.tensor_tensor(rk[:], rk[:], oh[:], ALU.mult))
            link(dve.tensor_reduce(slot[:], rk[:], AX_X, ALU.add))
            link(dve.tensor_copy(slot_i[:, 0, :], slot[:]))
            dve.tensor_scalar(slot_i[:, 1, :], slot_i[:, 0, :], P - 1, None, ALU.bitwise_and)
            link(dve.tensor_scalar(slot_i[:, 2, :], slot_i[:, 0, :], 7, None, ALU.logical_shift_right))
            link(dve.tensor_copy(slot_f[:], slot_i[:, 1:3, :]))
            for t in range(NTOK):
                dve.tensor_scalar(ohlo[:, t, :], iota_lo[:], slot_f[:, 0, t:t + 1], None, ALU.is_equal)
            link(dve.tensor_tensor(ohhi[:], iota_hi[:], slot_f[:, 1, :].unsqueeze(2).to_broadcast([P, NTOK, NT]), ALU.is_equal))
            dve.tensor_tensor(uv[:, :, 0, :], ohhi[:], iota_t[:], ALU.mult)
            dve.tensor_scalar(uv[:, :, 1, :], ohhi[:], iota_p[:, 0:1], None, ALU.mult).then_inc(v_lo, 1)
            link(dve.tensor_tensor(past[:], starts[:], cnt[:, 2:3, :].to_broadcast([P, NT, E]), ALU.is_ge))
            link(dve.tensor_reduce(exf[:], past[:], AX_X, ALU.add))
            dve.tensor_scalar(expert[:], exf[:], float(E - 1), None, ALU.min).then_inc(v_exp, 1)
            dve.wait_ge(t_tab, 1)
            link(dve.tensor_scalar(tabf[:], ps[:, 2, 0:NT], float(P), float(N), ALU.mult, ALU.add))
            link(dve.tensor_tensor(tab2[:], tabf[:], ps[:, 2, NT:2 * NT], ALU.add))
            dve.tensor_copy(table[:], tab2[:]).then_inc(v_tab, 1)

            def turned_h(m, q):
                j = 4 * m + 3 + q
                after(dve, "dve", t_th, j + 1)
                after(dve, "dve", t_y, j)
                dve.tensor_copy(hT[:, 4, :], ps[:, 5, 0:P])
                dve.tensor_copy(hT[0:LAST, 5, :], ps[0:LAST, 5, P:2 * P]).then_inc(v_hT, 1)

            def gated(m, q):
                j = 4 * m + 3 + q
                for half in range(2):
                    after(dve, "dve", a_sg, 2 * j + half + 1)
                    after(dve, "dve", t_gu, 4 * j + 2 * half + 2)
                    after(dve, "dve", t_th, j)
                    n = slice(HALF * half, HALF * half + HALF)
                    dve.tensor_tensor(hm[:, n], sg[:, n], ps[:, 2 * half + 1, 0:HALF], ALU.mult).then_inc(v_h, 1)

            def finish(m, q):
                j = 4 * m + 3 + q
                r = (3 + q) % RING
                after(dve, "dve", t_y, j + 1)
                after(dve, "dve", d_scat[r], 16 * (m + (3 + q) // RING))
                dve.scalar_tensor_tensor(out=og[:, r, :], in0=ps[:, 6, 0:H], scalar=tg[:, 1:2], in1=xg[:, r, 0:H],
                                         op0=ALU.mult, op1=ALU.add).then_inc(v_out, 1)

            def tile(m, q, first=False):
                if not first:
                    turned_h(m, q - 1)
                gated(m, q)
                if not first:
                    finish(m, q - 1)

            for j in range(3):
                tile(-1, j + 1, first=(j == 0))
            for q in range(4):
                tile(0, q)
            with dve.Fori(1, NT // 4, 1) as m:
                for q in range(4):
                    tile(m, q)
            m = NT // 4 - 1
            turned_h(m, 3)
            finish(m, 3)


def kernel(x, ctx_1024, g_xattn, g_ffn, L0_xattn_Wq, L0_xattn_bq, L0_xattn_Wk, L0_xattn_bk, L0_xattn_Wv,
           L0_xattn_bv, L0_ffn_router_w, L0_ffn_gate_w, L0_ffn_up_w, L0_ffn_down_w):
    import numpy as np
    import concourse.bacc as bacc
    from concourse.bass_utils import run_bass_kernel_spmd

    def arr(a):
        return np.ascontiguousarray(a)

    gate, up, down = (np.asarray(a) for a in (L0_ffn_gate_w, L0_ffn_up_w, L0_ffn_down_w))
    gu = np.stack([gate.reshape(E, 2, HALF, C, P), up.reshape(E, 2, HALF, C, P)], axis=2)
    gu = gu.transpose(0, 5, 4, 1, 2, 3).reshape(E, P, C * 4 * HALF)
    dT = down.transpose(0, 2, 1)
    cut = (CI - 1) * P
    arrays = {
        "x": x, "ctxT": np.asarray(ctx_1024).reshape(B * K, H).T,
        "g_x": np.asarray(g_xattn).reshape(1, 1), "g_f": np.asarray(g_ffn).reshape(1, 1),
        "WqT": np.concatenate([np.asarray(L0_xattn_Wq).T, np.asarray(L0_xattn_bq).reshape(H, 1)], axis=1),
        "WkT": np.concatenate([np.asarray(L0_xattn_Wk).T, np.asarray(L0_xattn_bk).reshape(H, 1)], axis=1),
        "Wv": L0_xattn_Wv, "bv": np.asarray(L0_xattn_bv).reshape(1, H),
        "WrT": np.asarray(L0_ffn_router_w).T, "Wgu": gu,
        "Wd": dT[:, :cut].reshape(E, CI - 1, P, H).transpose(0, 2, 1, 3).reshape(E, P, (CI - 1) * H),
        "WdL": dT[:, cut:],
    }
    arrays = {f"in_{k}": arr(a) for k, a in arrays.items()}
    nc = bacc.Bacc("TRN2", target_bir_lowering=False, num_devices=1)
    args = [nc.dram_tensor(k, a.shape, mybir.dt.from_np(a.dtype), kind="ExternalInput").ap() for k, a in arrays.items()]
    out = nc.dram_tensor("out", (N, H), F32, kind="ExternalOutput").ap()
    flamingo_moe(nc, *args, out)
    r = run_bass_kernel_spmd(nc, [arrays], core_ids=[0])
    return r.results[0]["out"].reshape(B, S, H)
```

```python
from contextlib import ExitStack

import concourse.bass as bass
from concourse import mybir

F32 = mybir.dt.float32
BF16 = mybir.dt.bfloat16
I32 = mybir.dt.int32
U32 = mybir.dt.uint32
ALU = mybir.AluOpType
ACT = mybir.ActivationFunctionType
AX_X = mybir.AxisListType.X

P = 128
B, S, H = 8, 256, 256
K = 120
N = B * S
E, I = 8, 704
C = H // P
TB = S // P
NTOK = N // P
NT = (N + E - 1 + E * (P - 1)) // P
HALF = I // 2
CI = (I + P - 1) // P
LAST = I - (CI - 1) * P
RING = 4
EPS = 1e-5
MAGIC = 0x5F3759DF
NORM = H ** -0.5


def flamingo_moe(nc, x, ctxT, g_x, g_f, WqT, WkT, Wv, bv, WrT, Wgu, Wd, WdL, out):
    with ExitStack() as stack:
        def sb(name, shape, dt=F32):
            return stack.enter_context(nc.sbuf_tensor(name, shape, dt))

        def sem(name):
            return stack.enter_context(nc.semaphore(name))

        rows = nc.dram_tensor("x1_rows", (N + 1, H), F32, kind="Internal").ap()

        wgu = sb("wgu", [P, E, C, 4, HALF])
        wd = sb("wd", [P, E, CI, H])
        ctx_sb = sb("ctx_sb", [P, C, B * K])
        wqT = sb("wqT", [P, C, H + 1])
        wkT = sb("wkT", [P, C, H + 1])
        wv = sb("wv", [P, C, H])
        wrT = sb("wrT", [P, C, E])
        bvb = sb("bvb", [P, H])
        gates = sb("gates", [P, 2])
        tg = sb("tg", [P, 2])
        tgn = sb("tgn", [P, 1])
        bvt = bvb
        wrc = sb("wrc", [P, C, E])
        mean_w = sb("mean_w", [P, P])
        ident = sb("ident", [P, P])
        ones_row = sb("ones_row", [1, P])
        tri = sb("tri", [P, P], BF16)
        ones_b = sb("ones_b", [P, P], BF16)
        iota_p = sb("iota_p", [P, 1])
        iota_lo = sb("iota_lo", [P, P], BF16)
        iota_hi = sb("iota_hi", [P, 1, NT])
        iota_t = sb("iota_t", [P, NTOK, 1])
        iota_e = sb("iota_e", [P, 1, E])
        starts = sb("starts", [P, NT, 1])
        zrow = sb("zrow", [1, H])
        MT = sb("MT", [P, C, H + 1])
        wqbk = sb("wqbk", [P, C + 1])
        A = sb("A", [P, C, B * K])
        brow = sb("brow", [P, B * K])
        V = sb("V", [P, B, H])
        xin = sb("xin", [P, NTOK, H])
        st1 = sb("st1", [P, NTOK, 6])
        mv1 = sb("mv1", [P, NTOK, 2])
        rs1 = sb("rs1", [P, NTOK])
        nm1 = sb("nm1", [P, NTOK])
        nwt = sb("nwt", [P, 4, NTOK])
        xn = sb("xn", [P, TB, H])
        xnT = sb("xnT", [P, C, S])
        negmax = sb("negmax", [P, NTOK])
        ssum = sb("ssum", [P, NTOK])
        rsum = sb("rsum", [P, NTOK])
        prob = sb("prob", [P, TB, K])
        pT = sb("pT", [K, S])
        x1 = sb("x1", [P, 2, TB, H])
        st2 = sb("st2", [P, NTOK, 6])
        mv2 = sb("mv2", [P, NTOK, 2])
        rs2 = sb("rs2", [P, 2, NTOK])
        x1T = wkT[:, :, 0:H]
        top8 = sb("top8", [P, NTOK, 8])
        idx8 = sb("idx8", [P, NTOK, 8], U32)
        pick = sb("pick", [P, NTOK])
        oh = sb("oh", [P, NTOK, E], BF16)
        cnt = sb("cnt", [P, 5, E])
        cnt_i = sb("cnt_i", [P, 2, E], I32)
        slot = sb("slot", [P, NTOK])
        slot_i = sb("slot_i", [P, 3, NTOK], I32)
        slot_f = sb("slot_f", [P, 2, NTOK])
        tabf = sb("tabf", [P, NT])
        stat = sb("stat", [P, 2, NT])
        tab2 = sb("tab2", [P, NT])
        table = sb("table", [P, NT], I32)
        exf = sb("exf", [P, NT])
        expert = sb("expert", [P, NT], I32)
        free_x = xin[:].rearrange("p t h -> p (t h)")
        free_a = A[:].rearrange("p c n -> p (c n)")

        def part(room, start, *dims):
            size = 1
            for d in dims:
                size *= d
            names = " ".join("abc"[:len(dims)])
            view = room[:, start:start + size]
            if len(dims) > 1:
                view = view.rearrange(f"p ({names}) -> p {names}", **dict(zip("abc", dims)))
            return view, start + size

        free_c = ctx_sb[:].rearrange("p c n -> p (c n)")
        ohhi, at = part(free_c, 0, NTOK, NT)
        ohlo, _ = part(free_c[:, at:at + NTOK * P // 2].bitcast(BF16), 0, NTOK, P)
        at += NTOK * P // 2
        uv, _ = part(free_c[:, at:at + NTOK * NT].bitcast(BF16), 0, NTOK, 2, NT)

        ohlo_f, _ = part(V[:].rearrange("p b h -> p (b h)"), 0, NTOK, P)
        rsel, _ = part(brow[:], 0, NTOK, 2 * NT)
        free_q = wqT[:].rearrange("p c n -> p (c n)")
        past, at = part(free_q, 0, NT, E)
        rk, at = part(free_q, at, NTOK, E)

        xg, at = part(free_x, 0, RING, H)
        og, at = part(free_x, at, RING, H)
        xh, at = part(free_x, at, 2, H)
        xhT, at = part(free_x, at, 2, C, P)
        sg, at = part(free_x, at, I)
        hm, at = part(free_a, 0, I)
        hT, at = part(free_a, at, CI, P)

        ps = stack.enter_context(nc.psum_tensor("ps", [P, 8, 512], F32))

        d_x = [sem(f"d_x{i}") for i in range(B)]
        d_wv, d_wq, d_ctx, d_sm, d_g = sem("d_wv"), sem("d_wq"), sem("d_ctx"), sem("d_sm"), sem("d_g")
        d_w = [sem(f"d_w{e}") for e in range(E)]
        w_ready = sem("w_ready")
        k_pool = sem("k_pool")
        a_tg, v_tg = sem("a_tg"), sem("v_tg")
        t_mt, a_mt = sem("t_mt"), sem("a_mt")
        t_v, v_v = sem("t_v"), sem("v_v")
        t_a, a_a = sem("t_a"), sem("a_a")
        t_br, a_br = sem("t_br"), sem("a_br")
        v_chain = sem("v_chain")
        v_st1 = sem("v_st1")
        a_xn, t_t1, a_xnT = sem("a_xn"), sem("t_t1"), sem("a_xnT")
        t_s, v_max, a_exp = sem("t_s"), sem("v_max"), sem("a_exp")
        t_t2, a_pT, t_pv = sem("t_t2"), sem("a_pT"), sem("t_pv")
        v_x1, v_aggr = sem("v_x1"), sem("v_aggr")
        d_row = [sem("d_row0"), sem("d_row1")]
        d_zrow = sem("d_zrow")
        t_t3, a_x1T = sem("t_t3"), sem("a_x1T")
        t_wr, v_wrc = sem("t_wr"), sem("v_wrc")
        a_lo, v_rsel, t_stat, v_stat = sem("a_lo"), sem("v_rsel"), sem("t_stat"), sem("v_stat")
        v_sort = sem("v_sort")
        t_lg, v_oh = sem("t_lg"), sem("v_oh")
        t_rk, v_lo, t_tab, v_tab, v_exp = sem("t_rk"), sem("v_lo"), sem("t_tab"), sem("v_tab"), sem("v_exp")
        d_gath = [sem(f"d_gath{r}") for r in range(RING)]
        d_scat = [sem(f"d_scat{r}") for r in range(RING)]
        a_xh, t_tx, a_xhT = sem("a_xh"), sem("t_tx"), sem("a_xhT")
        t_gu, a_sg, v_h = sem("t_gu"), sem("a_sg"), sem("v_h")
        t_th, a_hT, v_hT = sem("t_th"), sem("a_hT"), sem("v_hT")
        t_y, v_out = sem("t_y"), sem("v_out")
        idle = {n: sem(f"idle_{n}") for n in ("pe", "act", "dve", "pool", "sp")}

        def after(eng, name, s, value):
            if isinstance(value, int):
                if value > 0:
                    eng.wait_ge(s, value)
            else:
                eng.wait_ge(s, value)
                eng.sem_inc(idle[name], 1)

        block = stack.enter_context(nc.Block())

        @block.sync
        def _(sp):
            def ap(t, c):
                return t.rearrange("(c p) n -> p c n", c=c)

            sp.dma_start(wkT[:], ap(WkT, C)).then_inc(d_wq, 16)
            sp.dma_start(wqT[:], ap(WqT, C)).then_inc(d_wq, 16)
            sp.dma_start(ctx_sb[:], ap(ctxT, C)).then_inc(d_ctx, 16)
            xv = x.rearrange("b (t p) h -> b p t h", p=P)
            for b in range(B):
                if b == 2:
                    sp.dma_start(wv[:], ap(Wv, C)).then_inc(d_wv, 16)
                sp.dma_start(xin[:, TB * b:TB * b + TB, :], xv[b]).then_inc(d_x[b], 16)

            def expert_weights(e):
                sp.dma_start(wgu[:, e].rearrange("p c g n -> p (c g n)"), Wgu[e]).then_inc(d_w[e], 16)
                sp.dma_start(wd[:, e, 0:CI - 1, :].rearrange("p c n -> p (c n)"), Wd[e]).then_inc(d_w[e], 16)
                sp.dma_start(wd[0:LAST, e, CI - 1, :], WdL[e]).then_inc(d_w[e], 16)

            expert_weights(0)
            sp.wait_ge(k_pool, 1)
            sp.dma_start(rows[N:N + 1, :], zrow[:]).then_inc(d_zrow, 16)

            rv = rows[0:N].rearrange("(b t p) h -> b p t h", p=P, t=TB)

            for i in range(B):
                sp.wait_ge(v_x1, i + 1)
                sp.dma_start(rv[i], x1[:, i % 2]).then_inc(d_row[i % 2], 16)
                if i + 1 < E:
                    expert_weights(i + 1)
            for e in range(E):
                sp.wait_ge(d_w[e], 48)
                sp.sem_inc(w_ready, 1)

        @block.gpsimd
        def _(pool):
            kinds = [
                lambda: pool.memset(zrow[:], 0.0),
                lambda: pool.memset(ident[:], 0.0),
                lambda: pool.memset(tri[:], 1.0),
                lambda: pool.memset(ones_b[:], 1.0),
                lambda: pool.memset(ones_row[:], 1.0),
                lambda: pool.memset(mean_w[:], 1.0 / H),
            ]
            for make in kinds:
                make().then_inc(k_pool, 1)
            fl = dict(allow_small_or_imprecise_dtypes=True)
            pool.wait_ge(k_pool, 6)
            pool.affine_select(out=ident[:], in_=ident[:], compare_op=ALU.not_equal, fill=1.0, base=0,
                               pattern=[[-1, P]], channel_multiplier=1).then_inc(k_pool, 1)
            pool.affine_select(out=tri[:], in_=tri[:], compare_op=ALU.is_gt, fill=0.0, base=0,
                               pattern=[[1, P]], channel_multiplier=-1).then_inc(k_pool, 1)
            pool.iota(iota_p[:], pattern=[[0, 1]], base=0, channel_multiplier=1, **fl).then_inc(k_pool, 1)
            pool.iota(iota_lo[:], pattern=[[1, P]], base=0, channel_multiplier=0, **fl).then_inc(k_pool, 1)
            pool.iota(iota_e[:].rearrange("p a b -> p (a b)"), pattern=[[1, E]], base=0, channel_multiplier=0, **fl).then_inc(k_pool, 1)
            pool.iota(iota_hi[:].rearrange("p a b -> p (a b)"), pattern=[[1, NT]], base=0, channel_multiplier=0, **fl).then_inc(k_pool, 1)
            pool.iota(iota_t[:].rearrange("p a b -> p (a b)"), pattern=[[1, NTOK]], base=-NTOK, channel_multiplier=0, **fl).then_inc(k_pool, 1)
            pool.iota(starts[:].rearrange("p a b -> p (a b)"), pattern=[[P, NT]], base=0, channel_multiplier=0, **fl).then_inc(k_pool, 1)

            for par in range(2):
                pool.wait_ge(d_row[par], 16 * (B // 2))
            pool.wait_ge(d_zrow, 16)
            pool.wait_ge(v_tab, 1)

            idx = table

            def gather(j):
                pool.indirect_dma_start(
                    out=xg[:, j % RING, :], out_offset=None, in_=rows,
                    in_offset=bass.IndirectOffsetOnAxis(ap=idx[:, j:j + 1], axis=0)).then_inc(d_gath[j % RING], 16)

            def scatter(j):
                pool.indirect_dma_start(
                    out=out, out_offset=bass.IndirectOffsetOnAxis(ap=idx[:, j:j + 1], axis=0),
                    in_=og[:, j % RING, :], in_offset=None, bounds_check=N - 1,
                    oob_is_err=False).then_inc(d_scat[j % RING], 16)

            for j in range(RING):
                gather(j)
            for j in range(NT):
                pool.wait_ge(v_out, j + 1)
                if j + RING < NT:
                    gather(j + RING)
                scatter(j)
            for r in range(RING):
                pool.wait_ge(d_scat[r], 16 * len(range(r, NT, RING)))

        @block.scalar
        def _(act):
            act.dma_start(gates[:, 0:1], g_x.to_broadcast([P, 1])).then_inc(d_g, 16)
            act.dma_start(gates[:, 1:2], g_f.to_broadcast([P, 1])).then_inc(d_g, 16)
            act.dma_start(bvb[:], bv.to_broadcast([P, H])).then_inc(d_sm, 16)
            act.dma_start(wrT[:], WrT.rearrange("(c p) n -> p c n", c=C)).then_inc(d_sm, 16)
            act.wait_ge(d_g, 32)
            act.activation(tg[:], gates[:], ACT.Tanh).then_inc(a_tg, 1)
            act.wait_ge(t_mt, 1)
            for m in range(C):
                act.activation(MT[:, m, :], ps[:, 4 + m, 0:H + 1], ACT.Copy).then_inc(a_mt, 1)
            act.activation(wqbk[:, 0:C], ps[:, 4, 300:300 + C], ACT.Copy, scale=-1.0).then_inc(a_mt, 1)
            act.activation(wqbk[0:1, C:C + 1], ps[0:1, 5, 300:301], ACT.Copy, scale=-1.0).then_inc(a_mt, 1)
            def norm1(i):
                act.wait_ge(v_st1, 1 if i < 2 else 2)
                if i:
                    act.wait_ge(t_t1, i)
                for k in range(TB):
                    t = TB * i + k
                    ins = act.activation(xn[:, k, :], xin[:, t, :], ACT.Identity,
                                         scale=rs1[:, t:t + 1], bias=nm1[:, t:t + 1])
                ins.then_inc(a_xn, 1)

            def turned1(i):
                act.wait_ge(t_t1, i + 1)
                if i:
                    act.wait_ge(t_s, i)
                act.activation(xnT[:].rearrange("p c s -> p (c s)"), ps[:, 0, :], ACT.Copy).then_inc(a_xnT, 1)

            def exps(i):
                act.wait_ge(v_max, i + 1)
                if i:
                    act.wait_ge(t_t2, i)
                for k in range(TB):
                    t = TB * i + k
                    ins = act.activation(prob[:, k, :], ps[:, 2, K * k:K * k + K], ACT.Exp, scale=-1.0,
                                         bias=negmax[:, t:t + 1], accum_out=ssum[:, t:t + 1])
                ins.then_inc(a_exp, 1)

            def turned2(i):
                act.wait_ge(t_t2, i + 1)
                if i:
                    act.wait_ge(t_pv, i)
                act.activation(pT[:], ps[0:K, 3, 0:S], ACT.Copy).then_inc(a_pT, 1)

            def turned3(i):
                act.wait_ge(t_t3, i + 1)
                if i:
                    act.wait_ge(t_lg, i)
                act.activation(x1T, ps[:, 1, :].rearrange("p (c s) -> p c s", c=C), ACT.Copy).then_inc(a_x1T, 1)

            norm1(0)
            act.wait_ge(a_mt, C + 2)
            for q in range(4):
                n, m = q // 2, q % 2
                act.wait_ge(t_a, q + 1)
                act.activation(A[:, m, 480 * n:480 * n + 480], ps[:, q, 0:480], ACT.Identity, scale=-1.0,
                               bias=wqbk[:, m:m + 1]).then_inc(a_a, 1)
            for n in range(2):
                act.wait_ge(t_br, n + 1)
                act.activation(brow[0:1, 480 * n:480 * n + 480], ps[0:1, 6 + n, 0:480], ACT.Identity, scale=-1.0,
                               bias=wqbk[0:1, C:C + 1]).then_inc(a_br, 1)
            turned1(0)
            norm1(1)
            for i in range(B):
                exps(i)
                if i + 1 < B:
                    turned1(i + 1)
                if i:
                    turned3(i - 1)
                turned2(i)
                if i + 2 < B:
                    norm1(i + 2)
            turned3(B - 1)
            act.wait_ge(v_lo, 1)
            act.activation(ohlo_f, ohlo, ACT.Copy).then_inc(a_lo, 1)

            def gathered(m, q):
                j = 4 * m + 3 + q
                r = (3 + q) % RING
                after(act, "act", d_gath[r], 16 * (m + (3 + q) // RING + 1))
                after(act, "act", t_tx, j - 1)
                act.activation(xh[:, (3 + q) % 2, :], xg[:, r, 0:H], ACT.Identity,
                               scale=stat[:, 0, bass.ds(j, 1)], bias=stat[:, 1, bass.ds(j, 1)]).then_inc(a_xh, 1)

            def turned_x(m, q):
                j = 4 * m + 3 + q
                after(act, "act", t_tx, j + 1)
                after(act, "act", t_gu, 4 * (j - 1))
                act.activation(xhT[:, (3 + q) % 2].rearrange("p c t -> p (c t)"), ps[:, 7, 0:H],
                               ACT.Copy).then_inc(a_xhT, 1)

            def turned_h(m, q):
                j = 4 * m + 3 + q
                after(act, "act", t_th, j + 1)
                after(act, "act", t_y, j)
                act.activation(hT[:, 0:4, :].rearrange("p c t -> p (c t)"), ps[:, 4, :], ACT.Copy).then_inc(a_hT, 1)

            def silus(m, q):
                j = 4 * m + 3 + q
                for half in range(2):
                    after(act, "act", t_gu, 4 * j + 2 * half + 1)
                    after(act, "act", v_h, 2 * (j - 1) + half + 1)
                    act.activation(sg[:, HALF * half:HALF * half + HALF], ps[:, 2 * half, 0:HALF],
                                   ACT.Silu).then_inc(a_sg, 1)

            def tile(m, q, first=False, ahead1=True, ahead2=True):
                if not first:
                    turned_h(m, q - 1)
                if ahead1:
                    turned_x(m, q + 1)
                if ahead2:
                    gathered(m, q + 2)
                silus(m, q)

            act.wait_ge(v_stat, 1)
            gathered(-1, 1)
            turned_x(-1, 1)
            gathered(-1, 2)
            for j in range(3):
                tile(-1, j + 1, first=(j == 0))
            for q in range(4):
                tile(0, q)
            with act.Fori(1, NT // 4 - 1, 1) as m:
                for q in range(4):
                    tile(m, q)
            m = NT // 4 - 1
            for q in range(4):
                tile(m, q, ahead1=(4 * m + 3 + q + 1 < NT), ahead2=(4 * m + 3 + q + 2 < NT))
            turned_h(m, 3)

        @block.tensor
        def _(pe):
            pe.wait_ge(d_wq, 32)
            for m in range(C):
                for c in range(C):
                    pe.matmul(ps[:, 4 + m, 0:H + 1], wkT[:, c, P * m:P * m + P], wqT[:, c, :],
                              start=(c == 0), stop=(c == C - 1))
            for m in range(C):
                for c in range(C):
                    pe.matmul(ps[:, 4, 300 + m:301 + m], wqT[:, c, P * m:P * m + P], wkT[:, c, H:H + 1],
                              start=(c == 0), stop=(c == C - 1))
            for c in range(C):
                last = pe.matmul(ps[0:1, 5, 300:301], wqT[:, c, H:H + 1], wkT[:, c, H:H + 1],
                                 start=(c == 0), stop=(c == C - 1))
            last.then_inc(t_mt, 1)
            pe.wait_ge(d_ctx, 16)
            pe.wait_ge(a_mt, C + 2)
            for q in range(4):
                n, m = q // 2, q % 2
                for c in range(C):
                    last = pe.matmul(ps[:, q, 0:480], MT[:, c, P * m:P * m + P], ctx_sb[:, c, 480 * n:480 * n + 480],
                                     start=(c == 0), stop=(c == C - 1))
                last.then_inc(t_a, 1)
            for n in range(2):
                for c in range(C):
                    last = pe.matmul(ps[0:1, 6 + n, 0:480], MT[:, c, H:H + 1], ctx_sb[:, c, 480 * n:480 * n + 480],
                                     start=(c == 0), stop=(c == C - 1))
                last.then_inc(t_br, 1)
            pe.wait_ge(k_pool, 14)
            pe.wait_ge(d_sm, 32)
            for c in range(C):
                last = pe.matmul(ps[:, 5, 0:E], mean_w[:], wrT[:, c, :], start=(c == 0), stop=(c == C - 1))
            last.then_inc(t_wr, 1)

            def turn1(i):
                pe.wait_ge(a_xn, i + 1)
                if i:
                    pe.wait_ge(a_xnT, i)
                for k in range(TB):
                    for c in range(C):
                        last = pe.transpose(ps[:, 0, S * c + P * k:S * c + P * k + P],
                                            xn[:, k, P * c:P * c + P], ident[:])
                last.then_inc(t_t1, 1)

            def context(i):
                if i:
                    pe.wait_ge(v_v, i)
                for c in range(C):
                    last = pe.matmul(ps[0:K, 6, 0:H], ctx_sb[:, c, K * i:K * i + K], wv[:, c, :],
                                     start=(c == 0), stop=(c == C - 1))
                last.then_inc(t_v, 1)

            def scores(i):
                pe.wait_ge(a_xnT, i + 1)
                if i:
                    pe.wait_ge(a_exp, i)
                for k in range(TB):
                    for c in range(C):
                        pe.matmul(ps[:, 2, K * k:K * k + K], xnT[:, c, P * k:P * k + P],
                                  A[:, c, K * i:K * i + K], start=(c == 0), stop=False)
                    last = pe.matmul(ps[:, 2, K * k:K * k + K], ones_row[:], brow[0:1, K * i:K * i + K],
                                     start=False, stop=True)
                last.then_inc(t_s, 1)

            def turn2(i):
                pe.wait_ge(a_exp, i + 1)
                if i:
                    pe.wait_ge(a_pT, i)
                for k in range(TB):
                    last = pe.transpose(ps[0:K, 3, P * k:P * k + P], prob[:, k, :], ident[:])
                last.then_inc(t_t2, 1)

            def values(i):
                pe.wait_ge(a_pT, i + 1)
                pe.wait_ge(v_v, i + 1)
                if i:
                    pe.wait_ge(v_x1, i)
                for k in range(TB):
                    last = pe.matmul(ps[:, 4, H * k:H * k + H], pT[:, P * k:P * k + P], V[0:K, i, :],
                                     start=True, stop=True)
                last.then_inc(t_pv, 1)

            def turn3(i):
                pe.wait_ge(v_x1, i + 1)
                if i:
                    pe.wait_ge(a_x1T, i)
                for k in range(TB):
                    for c in range(C):
                        last = pe.transpose(ps[:, 1, S * c + P * k:S * c + P * k + P],
                                            x1[:, i % 2, k, P * c:P * c + P], ident[:])
                last.then_inc(t_t3, 1)

            def logits(i):
                pe.wait_ge(a_x1T, i + 1)
                pe.wait_ge(v_wrc, 1)
                if i:
                    pe.wait_ge(v_oh, i)
                for k in range(TB):
                    for c in range(C):
                        last = pe.matmul(ps[:, 5, E * k:E * k + E], x1T[:, c, P * k:P * k + P], wrc[:, c, :],
                                         start=(c == 0), stop=(c == C - 1))
                last.then_inc(t_lg, 1)

            pe.wait_ge(a_a, 4)
            turn1(0)
            pe.wait_ge(a_br, 2)
            pe.wait_ge(d_wv, 16)
            context(0)
            for i in range(B):
                scores(i)
                if i + 1 < B:
                    turn1(i + 1)
                if i:
                    turn3(i - 1)
                turn2(i)
                if i + 1 < B:
                    context(i + 1)
                values(i)
                if i:
                    logits(i - 1)
            turn3(B - 1)
            logits(B - 1)

            pe.wait_ge(v_sort, 1)
            for t in range(NTOK - 1):
                pe.matmul(ps[:, 0, E * (t + 1):E * NTOK].rearrange("p (t e) -> p t e", e=E), ones_b[:],
                          oh[:, t:t + 1, :].to_broadcast([P, NTOK - 1 - t, E]), start=(t == 0), stop=False,
                          skip_group_check=True)
            pe.matmul(ps[:, 0, 0:NTOK * E], tri[:], oh[:].rearrange("p t e -> p (t e)"), start=False, stop=True,
                      skip_group_check=True)
            for t in range(NTOK):
                last = pe.matmul(ps[:, 1, 0:E], ones_b[:], oh[:, t, :], start=(t == 0), stop=(t == NTOK - 1))
            last.then_inc(t_rk, 1)
            pe.wait_ge(v_lo, 1)
            for t in range(NTOK):
                last = pe.matmul(ps[:, 2, 0:2 * NT], ohlo[:, t, :], uv[:, t].rearrange("p a n -> p (a n)"),
                                 start=(t == 0), stop=(t == NTOK - 1))
            last.then_inc(t_tab, 1)
            pe.wait_ge(a_lo, 1)
            pe.wait_ge(v_rsel, 1)
            for t in range(NTOK):
                last = pe.matmul(ps[:, 3, 0:2 * NT], ohlo_f[:, t, :], rsel[:, t, :], start=(t == 0), stop=(t == NTOK - 1))
            last.then_inc(t_stat, 1)

            pe.wait_ge(v_exp, 1)

            def turn_x(m, q):
                j = 4 * m + 3 + q
                after(pe, "pe", a_xh, j + 1)
                after(pe, "pe", a_xhT, j)
                for c in range(C):
                    last = pe.transpose(ps[:, 7, P * c:P * c + P], xh[:, (3 + q) % 2, P * c:P * c + P], ident[:])
                last.then_inc(t_tx, 1)

            def turn_h(m, q):
                j = 4 * m + 3 + q
                after(pe, "pe", v_h, 2 * (j + 1))
                after(pe, "pe", a_hT, j)
                after(pe, "pe", v_hT, j)
                for c in range(CI):
                    rows_ = P if c < CI - 1 else LAST
                    last = pe.transpose(ps[0:rows_, 4 + c // 4, P * (c % 4):P * (c % 4) + P],
                                        hm[:, P * c:P * c + rows_], ident[:])
                last.then_inc(t_th, 1)

            def up(m, q):
                j = 4 * m + 3 + q
                e = pe.value_load(expert[0:1, bass.ds(j, 1)], min_val=0, max_val=E - 1)
                after(pe, "pe", w_ready, e + 1)
                after(pe, "pe", a_xhT, j + 1)
                for g in range(4):
                    for c in range(C):
                        last = pe.matmul(ps[:, g, 0:HALF], xhT[:, (3 + q) % 2, c, :],
                                         wgu[:, bass.ds(e, 1), c, g, :].rearrange("p o n -> p (o n)"),
                                         start=(c == 0), stop=(c == C - 1))
                    last.then_inc(t_gu, 1)

            def down(m, q):
                j = 4 * m + 3 + q
                e = pe.value_load(expert[0:1, bass.ds(j, 1)], min_val=0, max_val=E - 1)
                after(pe, "pe", a_hT, j + 1)
                after(pe, "pe", v_hT, j + 1)
                after(pe, "pe", v_out, j)
                for c in range(CI):
                    rows_ = P if c < CI - 1 else LAST
                    last = pe.matmul(ps[:, 6, 0:H], hT[0:rows_, c, :],
                                     wd[0:rows_, bass.ds(e, 1), c, :].rearrange("p o n -> p (o n)"),
                                     start=(c == 0), stop=(c == CI - 1))
                last.then_inc(t_y, 1)

            def tile(m, q, first=False, ahead=True):
                if not first:
                    turn_h(m, q - 1)
                if ahead:
                    turn_x(m, q + 1)
                up(m, q)
                if not first:
                    down(m, q - 1)

            turn_x(-1, 1)
            for j in range(3):
                tile(-1, j + 1, first=(j == 0))
            for q in range(4):
                tile(0, q)
            with pe.Fori(1, NT // 4 - 1, 1) as m:
                for q in range(4):
                    tile(m, q)
            m = NT // 4 - 1
            for q in range(4):
                tile(m, q, ahead=(4 * m + 3 + q + 1 < NT))
            turn_h(m, 3)
            down(m, 3)

        @block.vector
        def _(dve):
            chained = [0]

            def link(ins):
                chained[0] += 1
                ins.then_inc(v_chain, 1)
                dve.wait_ge(v_chain, chained[0])

            def newton(chain, var, mean, rs, nm, n):
                ve, y, a = nwt[:, 0, 0:n], nwt[:, 1, 0:n], nwt[:, 2, 0:n]
                chain(dve.tensor_scalar(ve, var, EPS, None, ALU.add))
                chain(dve.tensor_scalar(nwt[:, 3, 0:n].bitcast(I32), ve.bitcast(I32), 1, None, ALU.logical_shift_right))
                chain(dve.tensor_scalar(y.bitcast(I32), nwt[:, 3, 0:n].bitcast(I32), -1.0, float(MAGIC), ALU.mult, ALU.add))
                for step in range(3):
                    chain(dve.tensor_tensor(a, y, y, ALU.mult))
                    chain(dve.tensor_tensor(a, a, ve, ALU.mult))
                    chain(dve.tensor_scalar(a, a, -0.5, 1.5, ALU.mult, ALU.add))
                    chain(dve.tensor_tensor(rs if step == 2 else y, a, y, ALU.mult))
                return dve.scalar_tensor_tensor(out=nm, in0=mean, scalar=-1.0, in1=rs, op0=ALU.mult, op1=ALU.mult)

            for lo, hi in ((0, 2), (2, B)):
                for b in range(lo, hi):
                    dve.wait_ge(d_x[b], 16)
                    for k in range(TB):
                        ins = dve.bn_stats(st1[:, TB * b + k, :], xin[:, TB * b + k, :])
                link(ins)
                t = slice(TB * lo, TB * hi)
                for n in range(TB * lo, TB * hi):
                    ins = dve.bn_aggr(mv1[:, n, :], st1[:, n, :])
                link(ins)
                newton(link, mv1[:, t, 1], mv1[:, t, 0], rs1[:, t], nm1[:, t], TB * (hi - lo)).then_inc(v_st1, 1)
                if lo == 0:
                    dve.wait_ge(a_tg, 1)
                    link(dve.tensor_scalar(tgn[:], tg[:, 0:1], NORM, None, ALU.mult))
                    dve.wait_ge(d_sm, 32)
                    link(dve.tensor_scalar(bvt[:], bvb[:], tgn[:, 0:1], None, ALU.mult))
            dve.wait_ge(t_wr, 1)
            for c in range(C):
                ins = dve.tensor_tensor(wrc[:, c, :], wrT[:, c, :], ps[:, 5, 0:E], ALU.subtract)
            ins.then_inc(v_wrc, 1)

            def context(i):
                dve.wait_ge(t_v, i + 1)
                dve.scalar_tensor_tensor(out=V[0:K, i, :], in0=ps[0:K, 6, 0:H], scalar=tgn[0:K, 0:1], in1=bvt[0:K, :],
                                         op0=ALU.mult, op1=ALU.add).then_inc(v_v, 1)

            def minima(i):
                dve.wait_ge(t_s, i + 1)
                dve.tensor_reduce(negmax[:, TB * i:TB * i + TB], ps[:, 2, 0:TB * K].rearrange("p (t k) -> p t k", k=K),
                                  AX_X, ALU.min).then_inc(v_max, 1)

            def residual(i):
                dve.wait_ge(a_exp, i + 1)
                link(dve.reciprocal(rsum[:, TB * i:TB * i + TB], ssum[:, TB * i:TB * i + TB]))
                dve.wait_ge(t_pv, i + 1)
                if i >= 2:
                    dve.wait_ge(d_row[i % 2], 16 * (i // 2))
                    dve.wait_ge(t_t3, i - 1)
                for k in range(TB):
                    t = TB * i + k
                    ins = dve.scalar_tensor_tensor(out=x1[:, i % 2, k, :], in0=ps[:, 4, H * k:H * k + H],
                                                   scalar=rsum[:, t:t + 1], in1=xin[:, t, :],
                                                   op0=ALU.mult, op1=ALU.add)
                ins.then_inc(v_x1, 1)

            def statistics(i):
                dve.wait_ge(v_x1, i + 1)
                for k in range(TB):
                    ins = dve.bn_stats(st2[:, TB * i + k, :], x1[:, i % 2, k, :])
                link(ins)
                for k in range(TB):
                    ins = dve.bn_aggr(mv2[:, TB * i + k, :], st2[:, TB * i + k, :])
                ins.then_inc(v_aggr, 1)

            def route(i):
                dve.wait_ge(t_lg, i + 1)
                for k in range(TB):
                    ins = dve.max(top8[:, TB * i + k, :], ps[:, 5, E * k:E * k + E])
                link(ins)
                for k in range(TB):
                    ins = dve.max_index(idx8[:, TB * i + k, :], top8[:, TB * i + k, :], ps[:, 5, E * k:E * k + E])
                ins.then_inc(v_oh, 1)

            dve.wait_ge(k_pool, 14)
            context(0)
            for i in range(B):
                if i:
                    residual(i - 1)
                minima(i)
                if i:
                    statistics(i - 1)
                if i + 1 < B:
                    context(i + 1)
                if i:
                    route(i - 1)
            residual(B - 1)
            statistics(B - 1)
            route(B - 1)
            dve.wait_ge(v_oh, B)
            link(dve.tensor_copy(pick[:], idx8[:, :, 0]))
            dve.tensor_tensor(oh[:], iota_e[:].to_broadcast([P, NTOK, E]), pick[:].unsqueeze(2).to_broadcast([P, NTOK, E]),
                              ALU.is_equal).then_inc(v_sort, 1)
            dve.wait_ge(v_aggr, B)
            newton(link, mv2[:, :, 1], mv2[:, :, 0], rs2[:, 0, :], rs2[:, 1, :], NTOK).then_inc(v_aggr, 1)

            dve.wait_ge(v_sort, 1)
            dve.wait_ge(t_rk, 1)
            n_of, padded, ends, offs = cnt[:, 0, :], cnt[:, 1, :], cnt[:, 2, :], cnt[:, 3, :]
            link(dve.tensor_scalar(n_of, ps[:, 1, 0:E], 1.0, float(P - 1), ALU.max, ALU.add))
            link(dve.tensor_copy(cnt_i[:, 0, :], n_of))
            link(dve.tensor_scalar(cnt_i[:, 1, :], cnt_i[:, 0, :], 7, 7, ALU.logical_shift_right, ALU.logical_shift_left))
            link(dve.tensor_copy(padded, cnt_i[:, 1, :]))
            link(dve.memset(cnt[:, 4, :], 0.0))
            link(dve.tensor_tensor_scan(ends, padded, cnt[:, 4, :], 0.0, ALU.add, ALU.add))
            link(dve.tensor_tensor(offs, ends, padded, ALU.subtract))
            link(dve.tensor_tensor(rk[:], ps[:, 0, 0:NTOK * E].rearrange("p (t e) -> p t e", e=E),
                                   cnt[:, 3:4, :].to_broadcast([P, NTOK, E]), ALU.add))
            link(dve.tensor_tensor(rk[:], rk[:], oh[:], ALU.mult))
            link(dve.tensor_reduce(slot[:], rk[:], AX_X, ALU.add))
            link(dve.tensor_copy(slot_i[:, 0, :], slot[:]))
            dve.tensor_scalar(slot_i[:, 1, :], slot_i[:, 0, :], P - 1, None, ALU.bitwise_and)
            link(dve.tensor_scalar(slot_i[:, 2, :], slot_i[:, 0, :], 7, None, ALU.logical_shift_right))
            link(dve.tensor_copy(slot_f[:], slot_i[:, 1:3, :]))
            for t in range(NTOK):
                dve.tensor_scalar(ohlo[:, t, :], iota_lo[:], slot_f[:, 0, t:t + 1], None, ALU.is_equal)
            link(dve.tensor_tensor(ohhi[:], iota_hi[:].to_broadcast([P, NTOK, NT]), slot_f[:, 1, :].unsqueeze(2).to_broadcast([P, NTOK, NT]), ALU.is_equal))
            dve.tensor_tensor(uv[:, :, 0, :], ohhi[:], iota_t[:].to_broadcast([P, NTOK, NT]), ALU.mult)
            dve.tensor_scalar(uv[:, :, 1, :], ohhi[:], iota_p[:, 0:1], None, ALU.mult).then_inc(v_lo, 1)
            link(dve.tensor_tensor(past[:], starts[:].to_broadcast([P, NT, E]), cnt[:, 2:3, :].to_broadcast([P, NT, E]), ALU.is_ge))
            link(dve.tensor_reduce(exf[:], past[:], AX_X, ALU.add))
            dve.tensor_scalar(expert[:], exf[:], float(E - 1), None, ALU.min).then_inc(v_exp, 1)
            dve.wait_ge(t_tab, 1)
            link(dve.tensor_scalar(tabf[:], ps[:, 2, 0:NT], float(P), float(N), ALU.mult, ALU.add))
            link(dve.tensor_tensor(tab2[:], tabf[:], ps[:, 2, NT:2 * NT], ALU.add))
            dve.tensor_copy(table[:], tab2[:]).then_inc(v_tab, 1)
            dve.wait_ge(v_aggr, B + 1)
            for n in range(2):
                ins = dve.tensor_tensor(rsel[:, :, NT * n:NT * n + NT], ohhi,
                                        rs2[:, n, :].unsqueeze(2).to_broadcast([P, NTOK, NT]), ALU.mult)
            ins.then_inc(v_rsel, 1)
            dve.wait_ge(t_stat, 1)
            dve.tensor_copy(stat[:].rearrange("p a n -> p (a n)"), ps[:, 3, 0:2 * NT]).then_inc(v_stat, 1)

            def turned_h(m, q):
                j = 4 * m + 3 + q
                after(dve, "dve", t_th, j + 1)
                after(dve, "dve", t_y, j)
                dve.tensor_copy(hT[:, 4, :], ps[:, 5, 0:P])
                dve.tensor_copy(hT[0:LAST, 5, :], ps[0:LAST, 5, P:2 * P]).then_inc(v_hT, 1)

            def gated(m, q):
                j = 4 * m + 3 + q
                for half in range(2):
                    after(dve, "dve", a_sg, 2 * j + half + 1)
                    after(dve, "dve", t_gu, 4 * j + 2 * half + 2)
                    after(dve, "dve", t_th, j)
                    n = slice(HALF * half, HALF * half + HALF)
                    dve.tensor_tensor(hm[:, n], sg[:, n], ps[:, 2 * half + 1, 0:HALF], ALU.mult).then_inc(v_h, 1)

            def finish(m, q):
                j = 4 * m + 3 + q
                r = (3 + q) % RING
                after(dve, "dve", t_y, j + 1)
                after(dve, "dve", d_scat[r], 16 * (m + (3 + q) // RING))
                dve.scalar_tensor_tensor(out=og[:, r, :], in0=ps[:, 6, 0:H], scalar=tg[:, 1:2], in1=xg[:, r, 0:H],
                                         op0=ALU.mult, op1=ALU.add).then_inc(v_out, 1)

            def tile(m, q, first=False):
                if not first:
                    turned_h(m, q - 1)
                gated(m, q)
                if not first:
                    finish(m, q - 1)

            for j in range(3):
                tile(-1, j + 1, first=(j == 0))
            for q in range(4):
                tile(0, q)
            with dve.Fori(1, NT // 4, 1) as m:
                for q in range(4):
                    tile(m, q)
            m = NT // 4 - 1
            turned_h(m, 3)
            finish(m, 3)


def kernel(x, ctx_1024, g_xattn, g_ffn, L0_xattn_Wq, L0_xattn_bq, L0_xattn_Wk, L0_xattn_bk, L0_xattn_Wv,
           L0_xattn_bv, L0_ffn_router_w, L0_ffn_gate_w, L0_ffn_up_w, L0_ffn_down_w):
    import numpy as np
    import concourse.bacc as bacc
    from concourse.bass_utils import run_bass_kernel_spmd

    def arr(a):
        return np.ascontiguousarray(a)

    gate, up, down = (np.asarray(a) for a in (L0_ffn_gate_w, L0_ffn_up_w, L0_ffn_down_w))
    gu = np.stack([gate.reshape(E, 2, HALF, C, P), up.reshape(E, 2, HALF, C, P)], axis=2)
    gu = gu.transpose(0, 5, 4, 1, 2, 3).reshape(E, P, C * 4 * HALF)
    dT = down.transpose(0, 2, 1)
    cut = (CI - 1) * P
    arrays = {
        "x": x, "ctxT": np.asarray(ctx_1024).reshape(B * K, H).T,
        "g_x": np.asarray(g_xattn).reshape(1, 1), "g_f": np.asarray(g_ffn).reshape(1, 1),
        "WqT": np.concatenate([np.asarray(L0_xattn_Wq).T, np.asarray(L0_xattn_bq).reshape(H, 1)], axis=1),
        "WkT": np.concatenate([np.asarray(L0_xattn_Wk).T, np.asarray(L0_xattn_bk).reshape(H, 1)], axis=1),
        "Wv": L0_xattn_Wv, "bv": np.asarray(L0_xattn_bv).reshape(1, H),
        "WrT": np.asarray(L0_ffn_router_w).T, "Wgu": gu,
        "Wd": dT[:, :cut].reshape(E, CI - 1, P, H).transpose(0, 2, 1, 3).reshape(E, P, (CI - 1) * H),
        "WdL": dT[:, cut:],
    }
    arrays = {f"in_{k}": arr(a) for k, a in arrays.items()}
    nc = bacc.Bacc("TRN2", target_bir_lowering=False, num_devices=1)
    args = [nc.dram_tensor(k, a.shape, mybir.dt.from_np(a.dtype), kind="ExternalInput").ap() for k, a in arrays.items()]
    out = nc.dram_tensor("out", (N, H), F32, kind="ExternalOutput").ap()
    flamingo_moe(nc, *args, out)
    r = run_bass_kernel_spmd(nc, [arrays], core_ids=[0])
    return r.results[0]["out"].reshape(B, S, H)
```

```python
from contextlib import ExitStack

import concourse.bass as bass
from concourse import mybir

F32 = mybir.dt.float32
F32R = mybir.dt.float32r
BF16 = mybir.dt.bfloat16
I32 = mybir.dt.int32
U32 = mybir.dt.uint32
ALU = mybir.AluOpType
ACT = mybir.ActivationFunctionType
AX_X = mybir.AxisListType.X

P = 128
B, S, H = 8, 256, 256
K = 120
N = B * S
E, I = 8, 704
C = H // P
TB = S // P
NTOK = N // P
NT = (N + E - 1 + E * (P - 1)) // P
HALF = I // 2
CI = (I + P - 1) // P
LAST = I - (CI - 1) * P
RING = 4
SEATS = 8
AHEAD = 6
GU = C * 4 * HALF
SPLIT = 3
SHARE = 3
RAW = 2
SURE = N // P
EPS = 1e-5
MAGIC = 0x5F3759DF
NORM = H ** -0.5


def flamingo_moe(nc, x, ctxT, g_x, g_f, WqT, WkT, Wv, bv, WrT, Wgu, Wd, WdL, out):
    with ExitStack() as stack:
        def sb(name, shape, dt=F32):
            return stack.enter_context(nc.sbuf_tensor(name, shape, dt))

        def sem(name):
            return stack.enter_context(nc.semaphore(name))

        rows = nc.dram_tensor("x1_rows", (N + 1, H), F32, kind="Internal").ap()

        raw_gu = sb("raw_gu", [P, RAW, GU])
        both = sb("both", [P, C * B * K + CI * H])
        ctx_sb = both[:, 0:C * B * K].rearrange("p (c n) -> p c n", c=C)
        raw_d = both[:, C * B * K - CI * H:].rearrange("p (r c n) -> p r c n", r=2, c=CI)
        wgu = sb("wgu", [P, SPLIT, 2, C, 4, HALF], F32R)
        wd = sb("wd", [P, SPLIT, 2, CI, H], F32R)
        xhT = sb("xhT", [P, 2, 2, C, P], F32R)
        hT = sb("hT", [P, 2, CI, P], F32R)
        wqT = sb("wqT", [P, C, H + 1])
        wkT = sb("wkT", [P, C, H + 1])
        wv = sb("wv", [P, C, H])
        wrT = sb("wrT", [P, C, E])
        bvb = sb("bvb", [P, H])
        gates = sb("gates", [P, 2])
        tg = sb("tg", [P, 2])
        tgn = sb("tgn", [P, 1])
        bvt = bvb
        wrc = sb("wrc", [P, C, E])
        ident = sb("ident", [P, P])
        ones_row = sb("ones_row", [1, P])
        tri = sb("tri", [P, P], BF16)
        ones_b = sb("ones_b", [P, P], BF16)
        iota_p = sb("iota_p", [P, 1])
        iota_lo = sb("iota_lo", [P, P], BF16)
        iota_hi = sb("iota_hi", [P, 1, NT])
        iota_t = sb("iota_t", [P, NTOK, 1])
        iota_e = sb("iota_e", [P, 1, E])
        starts = sb("starts", [P, NT, 1])
        MT = sb("MT", [P, C, H + 1])
        wqbk = sb("wqbk", [P, C + 1])
        A = sb("A", [P, C, B * K])
        brow = sb("brow", [P, B * K])
        V = sb("V", [P, B, H])
        xin = sb("xin", [P, NTOK, H])
        st1 = sb("st1", [P, NTOK, 6])
        mv1 = sb("mv1", [P, NTOK, 2])
        rs1 = sb("rs1", [P, NTOK])
        nm1 = sb("nm1", [P, NTOK])
        nwt = sb("nwt", [P, 4, NTOK])
        xn = sb("xn", [P, TB, H])
        xnT = sb("xnT", [P, C, S])
        negmax = sb("negmax", [P, NTOK])
        ssum = sb("ssum", [P, NTOK])
        rsum = sb("rsum", [P, NTOK])
        prob = sb("prob", [P, TB, K])
        pT = sb("pT", [K, S])
        x1 = sb("x1", [P, 2, TB, H])
        st2 = sb("st2", [P, NTOK, 6])
        mv2 = sb("mv2", [P, NTOK, 2])
        rs2 = sb("rs2", [P, 2, NTOK])
        x1T = wkT[:, :, 0:H]
        pick = sb("pick", [P, NTOK])
        oh = sb("oh", [P, NTOK + 1, E], BF16)
        cnt = sb("cnt", [P, 5, E])
        cnt_i = sb("cnt_i", [P, 2, E], I32)
        slot = sb("slot", [P, NTOK])
        slot_i = sb("slot_i", [P, 3, NTOK], I32)
        used = sb("used", [P, 1], I32)
        turn = sb("turn", [P, NT], I32)
        r3 = sb("r3", [P, NTOK, 3, 2], BF16)
        stat = sb("stat", [P, 2, NT])
        table = sb("table", [P, NT], I32)
        expert = sb("expert", [P, NT], I32)
        free_x = xin[:].rearrange("p t h -> p (t h)")
        free_a = A[:].rearrange("p c n -> p (c n)")

        def part(room, start, *dims):
            size = 1
            for d in dims:
                size *= d
            names = " ".join("abc"[:len(dims)])
            view = room[:, start:start + size]
            if len(dims) > 1:
                view = view.rearrange(f"p ({names}) -> p {names}", **dict(zip("abc", dims)))
            return view, start + size

        free_c = both[:, 0:C * B * K]
        ohhi, at = part(free_c, 0, NTOK, NT)
        ohlo, _ = part(free_c[:, at:at + NTOK * P // 2].bitcast(BF16), 0, NTOK, P)
        at += NTOK * P // 2
        uv, _ = part(free_c[:, at:at + NTOK * NT].bitcast(BF16), 0, NTOK, 2, NT)

        rsel, _ = part(V[:].rearrange("p b h -> p (b h)")[:, 0:NTOK * 3 * NT].bitcast(BF16), 0, NTOK, 6, NT)
        mean_w = V[:, B - 1, 0:P]
        free_m = MT[:].rearrange("p c n -> p (c n)")
        top8, at = part(free_m, 0, NTOK, 8)
        idx8, _ = part(free_m[:, at:at + NTOK * 8].bitcast(U32), 0, NTOK, 8)
        free_q = wqT[:].rearrange("p c n -> p (c n)")
        past, at = part(free_q, 0, NT, E)
        rk, at = part(free_q, at, NTOK, E)

        xg, at = part(free_x, 0, SEATS, H)
        og, at = part(free_x, at, RING, H)
        sg, at = part(free_x, at, I)
        hm, at = part(free_a, 0, I)
        xh, at = part(free_a, at, 2, H)
        slot_f, at = part(free_a, at, 2, NTOK)
        tabf, at = part(free_a, at, NT)
        tab2, at = part(free_a, at, NT)
        exf, at = part(free_a, at, NT)
        trf, at = part(free_a, at, 2, NT)
        rem, at = part(free_a, at, 2, NTOK, 2)

        def seat(j):
            return xg[:, bass.ds(j % SEATS, 1), :].rearrange("p o h -> p (o h)")

        ps = stack.enter_context(nc.psum_tensor("ps", [P, 8, 512], F32))

        d_x = [sem(f"d_x{i}") for i in range(B)]
        d_wv, d_wq, d_ctx, d_sm, d_g = sem("d_wv"), sem("d_wq"), sem("d_ctx"), sem("d_sm"), sem("d_g")
        d_gu, d_d = [sem(f"d_gu{e}") for e in range(E)], [sem(f"d_d{e}") for e in range(E)]
        gu_ready, d_ready = sem("gu_ready"), sem("d_ready")
        a_hg, a_hd = sem("a_hg"), sem("a_hd")
        p_lg, p_ld = sem("p_lg"), sem("p_ld")
        k_pool = sem("k_pool")
        a_tg = sem("a_tg")
        t_mt, a_mt = sem("t_mt"), sem("a_mt")
        t_v, v_v = sem("t_v"), sem("v_v")
        t_a, a_a = sem("t_a"), sem("a_a")
        t_br, a_br = sem("t_br"), sem("a_br")
        v_chain = sem("v_chain")
        v_st1 = sem("v_st1")
        v_xn, t_t1, a_xnT = sem("v_xn"), sem("t_t1"), sem("a_xnT")
        t_s, v_max, a_exp = sem("t_s"), sem("v_max"), sem("a_exp")
        t_t2, a_pT, t_pv = sem("t_t2"), sem("a_pT"), sem("t_pv")
        v_x1, v_aggr = sem("v_x1"), sem("v_aggr")
        d_row = [sem("d_row0"), sem("d_row1")]
        d_zrow = sem("d_zrow")
        t_t3, a_x1T = sem("t_t3"), sem("a_x1T")
        t_wr, v_wrc = sem("t_wr"), sem("v_wrc")
        p_chain = sem("p_chain")
        v_guess, p_r3 = sem("v_guess"), sem("p_r3")
        v_slot, p_lo = sem("v_slot"), sem("p_lo")
        v_rsel, t_stat, v_stat = sem("v_rsel"), sem("t_stat"), sem("v_stat")
        v_sort = sem("v_sort")
        t_lg, v_oh = sem("t_lg"), sem("v_oh")
        t_rk, v_lo, t_tab, v_tab, p_exp = sem("t_rk"), sem("v_lo"), sem("t_tab"), sem("v_tab"), sem("p_exp")
        d_gath = [sem(f"d_gath{r}") for r in range(RING)]
        d_scat = [sem(f"d_scat{r}") for r in range(RING)]
        a_xh, t_tx, a_xhT, v_xhT = sem("a_xh"), sem("t_tx"), sem("a_xhT"), sem("v_xhT")
        t_gu, a_sg, v_h = sem("t_gu"), sem("a_sg"), sem("v_h")
        t_th, a_hT, v_hT = sem("t_th"), sem("a_hT"), sem("v_hT")
        t_y, v_out = sem("t_y"), sem("v_out")
        idle = {n: sem(f"idle_{n}") for n in ("pe", "act", "dve", "pool", "sp")}

        def after(eng, name, s, value):
            if isinstance(value, int):
                if value > 0:
                    eng.wait_ge(s, value)
            else:
                eng.wait_ge(s, value)
                eng.sem_inc(idle[name], 1)

        def every_tile(eng, name, tile, drain):
            for j in range(7):
                tile(j // 4 - 1 if j < 3 else 0, j + 1 if j < 3 else j - 3, first=(j == 0))
            with eng.Fori(1, (SURE - 3) // 4, 1) as m:
                for q in range(4):
                    tile(m, q)
            for j in range(3 + 4 * ((SURE - 3) // 4), SURE):
                tile((j - 3) // 4, (j - 3) % 4)
            n_used = eng.value_load(used[0:1, 0:1], min_val=SURE, max_val=NT)
            for j in range(SURE, NT + 1):
                if j < NT:
                    with eng.If(n_used > j):
                        tile((j - 3) // 4, (j - 3) % 4, ahead1=(j + 1 < NT), ahead2=(j + 2 < NT))
                        eng.sem_inc(idle[name], 1)
                with eng.If(n_used == j):
                    drain((j - 4) // 4, (j - 4) % 4)

        def guess(eng, chain, var, n):
            ve, y = nwt[:, 0, 0:n], nwt[:, 1, 0:n]
            chain(eng.tensor_scalar(ve, var, EPS, None, ALU.add))
            chain(eng.tensor_scalar(nwt[:, 3, 0:n].bitcast(I32), ve.bitcast(I32), 1, None, ALU.logical_shift_right))
            return eng.tensor_scalar(y.bitcast(I32), nwt[:, 3, 0:n].bitcast(I32), -1.0, float(MAGIC), ALU.mult, ALU.add)

        def newton(eng, chain, mean, rs, nm, n):
            ve, y, a = nwt[:, 0, 0:n], nwt[:, 1, 0:n], nwt[:, 2, 0:n]
            for step in range(3):
                chain(eng.tensor_tensor(a, y, y, ALU.mult))
                chain(eng.tensor_tensor(a, a, ve, ALU.mult))
                chain(eng.tensor_scalar(a, a, -0.5, 1.5, ALU.mult, ALU.add))
                chain(eng.tensor_tensor(rs if step == 2 else y, a, y, ALU.mult))
            chain(eng.tensor_tensor(nm, mean, rs, ALU.mult))
            return eng.tensor_scalar(nm, nm, -1.0, None, ALU.mult)

        block = stack.enter_context(nc.Block())

        @block.sync
        def _(sp):
            def ap(t, c):
                return t.rearrange("(c p) n -> p c n", c=c)

            sp.dma_start(wkT[:], ap(WkT, C)).then_inc(d_wq, 16)
            sp.dma_start(wqT[:], ap(WqT, C)).then_inc(d_wq, 16)
            sp.dma_start(ctx_sb, ap(ctxT, C)).then_inc(d_ctx, 16)
            xv = x.rearrange("b (t p) h -> b p t h", p=P)
            for b in range(B):
                if b == 2:
                    sp.dma_start(wv[:], ap(Wv, C)).then_inc(d_wv, 16)
                sp.dma_start(xin[:, TB * b:TB * b + TB, :], xv[b]).then_inc(d_x[b], 16)

            def load_gu(e):
                if e >= RAW:
                    sp.wait_ge(a_hg, e - RAW + 1)
                    sp.wait_ge(p_lg, e - RAW + 1)
                sp.dma_start(raw_gu[:, e % RAW], Wgu[e]).then_inc(d_gu[e], 16)

            def load_d(e):
                if e == SPLIT + 1:
                    sp.wait_ge(t_stat, 1)
                elif e:
                    sp.wait_ge(a_hd, e if e <= SPLIT else e - 1)
                    sp.wait_ge(p_ld, e if e <= SPLIT else e - 1)
                place = raw_d[:, 1 if e <= SPLIT else e % 2]
                sp.dma_start(place[:, 0:CI - 1].rearrange("p c n -> p (c n)"), Wd[e]).then_inc(d_d[e], 16)
                sp.dma_start(place[0:LAST, CI - 1, :], WdL[e]).then_inc(d_d[e], 16)

            def arrived_gu(e):
                sp.wait_ge(d_gu[e], 16)
                sp.sem_inc(gu_ready, 1)

            def arrived_d(e):
                sp.wait_ge(d_d[e], 32)
                sp.sem_inc(d_ready, 1)

            load_gu(0)
            load_d(0)
            load_gu(1)
            for e in range(SPLIT + 1):
                arrived_gu(e)
                if e:
                    load_d(e)
                arrived_d(e)
                if e < SPLIT:
                    load_gu(e + RAW)
            for e in range(SPLIT + 1, E):
                if e >= SPLIT + RAW:
                    load_gu(e)
                load_d(e)
                arrived_gu(e)
                arrived_d(e)

        @block.gpsimd
        def _(pool):
            kinds = [
                lambda: pool.memset(ident[:], 0.0),
                lambda: pool.memset(tri[:], 1.0),
                lambda: pool.memset(ones_b[:], 1.0),
                lambda: pool.memset(ones_row[:], 1.0),
                lambda: pool.memset(mean_w, 1.0 / H),
            ]
            for make in kinds:
                make().then_inc(k_pool, 1)
            fl = dict(allow_small_or_imprecise_dtypes=True)
            pool.wait_ge(k_pool, 5)
            pool.affine_select(out=ident[:], in_=ident[:], compare_op=ALU.not_equal, fill=1.0, base=0,
                               pattern=[[-1, P]], channel_multiplier=1).then_inc(k_pool, 1)
            pool.affine_select(out=tri[:], in_=tri[:], compare_op=ALU.is_gt, fill=0.0, base=0,
                               pattern=[[1, P]], channel_multiplier=-1).then_inc(k_pool, 1)
            pool.iota(iota_p[:], pattern=[[0, 1]], base=0, channel_multiplier=1, **fl).then_inc(k_pool, 1)
            pool.iota(iota_lo[:], pattern=[[1, P]], base=0, channel_multiplier=0, **fl).then_inc(k_pool, 1)
            pool.iota(iota_e[:].rearrange("p a b -> p (a b)"), pattern=[[1, E]], base=0, channel_multiplier=0, **fl).then_inc(k_pool, 1)
            pool.iota(iota_hi[:].rearrange("p a b -> p (a b)"), pattern=[[1, NT]], base=0, channel_multiplier=0, **fl).then_inc(k_pool, 1)
            pool.iota(iota_t[:].rearrange("p a b -> p (a b)"), pattern=[[1, NTOK]], base=-NTOK, channel_multiplier=0, **fl).then_inc(k_pool, 1)
            pool.iota(starts[:].rearrange("p a b -> p (a b)"), pattern=[[P, NT]], base=0, channel_multiplier=0, **fl).then_inc(k_pool, 1)

            def low_gu(slot, raw):
                for c in range(C):
                    hi = wgu[:, slot, 0, c].rearrange("p o g n -> p (o g n)").bitcast(F32)
                    lo = wgu[:, slot, 1, c].rearrange("p o g n -> p (o g n)")
                    src = raw_gu[:, raw, GU // C * c:GU // C * (c + 1)].rearrange("p o n -> p (o n)")
                    ins = pool.tensor_tensor(lo, src, hi, ALU.subtract)
                ins.then_inc(p_lg, 1)

            def low_d(slot, raw=slice(1, 2)):
                pool.tensor_tensor(wd[:, slot, 1, 0:CI - 1, :].rearrange("p o c n -> p (o c n)"),
                                   raw_d[:, raw, 0:CI - 1, :].rearrange("p r c n -> p (r c n)"),
                                   wd[:, slot, 0, 0:CI - 1, :].rearrange("p o c n -> p (o c n)").bitcast(F32),
                                   ALU.subtract)
                pool.tensor_tensor(wd[0:LAST, slot, 1, CI - 1, :].rearrange("p o n -> p (o n)"),
                                   raw_d[0:LAST, raw, CI - 1, :].rearrange("p r n -> p (r n)"),
                                   wd[0:LAST, slot, 0, CI - 1, :].rearrange("p o n -> p (o n)").bitcast(F32),
                                   ALU.subtract).then_inc(p_ld, 1)

            def low_first(e):
                pool.wait_ge(a_hg, e + 1)
                low_gu(slice(e, e + 1), slice(e % RAW, e % RAW + 1))
                pool.wait_ge(a_hd, e + 1)
                low_d(slice(e, e + 1))

            for e in range(SPLIT - 1):
                low_first(e)

            linked = [0]

            def link(ins):
                linked[0] += 1
                ins.then_inc(p_chain, 1)
                pool.wait_ge(p_chain, linked[0])

            pool.wait_ge(v_guess, 1)
            link(newton(pool, link, mv2[:, :, 0], rs2[:, 0, :], rs2[:, 1, :], NTOK))
            for n in range(2):
                ins = pool.tensor_copy(rem[:, 0, :, n], rs2[:, n, :])
            link(ins)
            link(pool.tensor_copy(r3[:, :, 0, :], rem[:, 0]))
            link(pool.tensor_tensor(rem[:, 1], rem[:, 0], r3[:, :, 0, :], ALU.subtract))
            link(pool.tensor_copy(r3[:, :, 1, :], rem[:, 1]))
            link(pool.tensor_tensor(rem[:, 0], rem[:, 1], r3[:, :, 1, :], ALU.subtract))
            pool.tensor_copy(r3[:, :, 2, :], rem[:, 0]).then_inc(p_r3, 1)

            pool.wait_ge(v_slot, 1)
            for t in range(NTOK - SHARE, NTOK):
                ins = pool.tensor_scalar(ohlo[:, t, :], iota_lo[:], slot_f[:, 0, t:t + 1], None, ALU.is_equal)
            ins.then_inc(p_lo, 1)
            width = E
            while width > 2:
                width //= 2
                link(pool.tensor_tensor(past[:, :, 0:width], past[:, :, 0:width], past[:, :, width:2 * width], ALU.add))
            link(pool.tensor_tensor(exf[:], past[:, :, 0], past[:, :, 1], ALU.add))
            link(pool.tensor_scalar(exf[:], exf[:], float(E - 1), None, ALU.min))
            pool.memset(trf[:, 1, 0:1], 0.0)
            pool.tensor_tensor(trf[:, 0, 1:NT], exf[:, 1:NT], exf[:, 0:NT - 1], ALU.subtract)
            link(pool.tensor_scalar(trf[:, 1, 1:NT], exf[:, 0:NT - 1], float(E - 1 - SPLIT), None, ALU.is_le))
            link(pool.tensor_tensor(trf[:, 1, 1:NT], trf[:, 0, 1:NT], trf[:, 1, 1:NT], ALU.mult))
            pool.tensor_copy(turn[:], trf[:, 1, :])
            pool.tensor_copy(expert[:], exf[:])
            link(pool.tensor_scalar(used[:], cnt[:, 2, E - 1:E], 1.0 / P, None, ALU.mult))
            pool.sem_inc(p_exp, 1)

            for par in range(2):
                pool.wait_ge(d_row[par], 16 * (B // 2))
            pool.wait_ge(d_zrow, 16)
            pool.wait_ge(v_tab, 1)

            def gather(j):
                pool.indirect_dma_start(
                    out=xg[:, j % SEATS, :], out_offset=None, in_=rows,
                    in_offset=bass.IndirectOffsetOnAxis(ap=table[:, j:j + 1], axis=0)).then_inc(d_gath[j % RING], 16)

            def scatter(j):
                pool.indirect_dma_start(
                    out=out, out_offset=bass.IndirectOffsetOnAxis(ap=table[:, j:j + 1], axis=0),
                    in_=og[:, j % RING, :], in_offset=None, bounds_check=N - 1,
                    oob_is_err=False).then_inc(d_scat[j % RING], 16)

            def tile(j):
                if 0 < j < NT - 1:
                    now = pool.value_load(turn[0:1, j:j + 1], min_val=0, max_val=1)
                    with pool.If(now > 0):
                        e = pool.value_load(expert[0:1, j - 1:j], min_val=0, max_val=E - 1 - SPLIT)
                        after(pool, "pool", a_hg, e + SPLIT + 1)
                        low_gu(bass.ds(e % SPLIT, 1), bass.ds((e + SPLIT) % RAW, 1))
                        after(pool, "pool", a_hd, e + SPLIT + 1)
                        low_d(bass.ds(e % SPLIT, 1), bass.ds((e + SPLIT) % 2, 1))
                pool.wait_ge(v_out, j + 1)
                if j + AHEAD < NT:
                    gather(j + AHEAD)
                scatter(j)

            for j in range(AHEAD):
                if j == RING:
                    low_first(SPLIT - 1)
                if j >= RING:
                    pool.wait_ge(a_xh, j - RING + 1)
                gather(j)
            for j in range(SURE):
                tile(j)
            n_used = pool.value_load(used[0:1, 0:1], min_val=SURE, max_val=NT)
            for j in range(SURE, NT + 1):
                if j < NT:
                    with pool.If(n_used > j):
                        tile(j)
                with pool.If(n_used == j):
                    for r in range(RING):
                        pool.wait_ge(d_scat[r], 16 * len(range(r, j, RING)))
                    pool.sem_inc(idle["pool"], 1)

        @block.scalar
        def _(act):
            rv = rows[0:N].rearrange("(b t p) h -> b p t h", p=P, t=TB)
            act.dma_start(gates[:, 0:1], g_x.to_broadcast([P, 1])).then_inc(d_g, 16)
            act.dma_start(gates[:, 1:2], g_f.to_broadcast([P, 1])).then_inc(d_g, 16)
            act.dma_start(bvb[:], bv.to_broadcast([P, H])).then_inc(d_sm, 16)
            act.dma_start(wrT[:], WrT.rearrange("(c p) n -> p c n", c=C)).then_inc(d_sm, 16)
            act.wait_ge(d_g, 32)
            act.activation(tg[:], gates[:], ACT.Tanh).then_inc(a_tg, 1)
            act.wait_ge(t_mt, 1)
            for m in range(C):
                act.activation(MT[:, m, :], ps[:, 4 + m, 0:H + 1], ACT.Copy).then_inc(a_mt, 1)
            act.activation(wqbk[:, 0:C], ps[:, 4, 300:300 + C], ACT.Copy, scale=-1.0).then_inc(a_mt, 1)
            act.activation(wqbk[0:1, C:C + 1], ps[0:1, 5, 300:301], ACT.Copy, scale=-1.0).then_inc(a_mt, 1)
            def turned1(i):
                act.wait_ge(t_t1, i + 1)
                if i:
                    act.wait_ge(t_s, i)
                act.activation(xnT[:].rearrange("p c s -> p (c s)"), ps[:, 0, :], ACT.Copy).then_inc(a_xnT, 1)

            def exps(i):
                act.wait_ge(v_max, i + 1)
                if i:
                    act.wait_ge(t_t2, i)
                for k in range(TB):
                    t = TB * i + k
                    ins = act.activation(prob[:, k, :], ps[:, 2 + 5 * (i % 2), K * k:K * k + K], ACT.Exp, scale=-1.0,
                                         bias=negmax[:, t:t + 1], accum_out=ssum[:, t:t + 1])
                ins.then_inc(a_exp, 1)

            def turned2(i):
                act.wait_ge(t_t2, i + 1)
                if i:
                    act.wait_ge(t_pv, i)
                act.activation(pT[:], ps[0:K, 3, 0:S], ACT.Copy).then_inc(a_pT, 1)

            def turned3(i):
                act.wait_ge(t_t3, i + 1)
                if i:
                    act.wait_ge(t_lg, i)
                act.activation(x1T, ps[:, 1, :].rearrange("p (c s) -> p c s", c=C), ACT.Copy).then_inc(a_x1T, 1)

            def high(src, dst):
                return act.activation(dst, src, ACT.Copy)

            def high_gu(slot, raw, c):
                return high(raw_gu[:, raw, GU // C * c:GU // C * (c + 1)].rearrange("p o n -> p (o n)"),
                            wgu[:, slot, 0, c].rearrange("p o g n -> p (o g n)"))

            def high_d(slot, raw=slice(1, 2)):
                high(raw_d[:, raw, 0:CI - 1, :].rearrange("p r c n -> p (r c n)"),
                     wd[:, slot, 0, 0:CI - 1, :].rearrange("p o c n -> p (o c n)"))
                high(raw_d[0:LAST, raw, CI - 1, :].rearrange("p r n -> p (r n)"),
                     wd[0:LAST, slot, 0, CI - 1, :].rearrange("p o n -> p (o n)")).then_inc(a_hd, 1)

            act.wait_ge(a_mt, C + 2)
            for q in range(4):
                n, m = q // 2, q % 2
                act.wait_ge(t_a, q + 1)
                act.activation(A[:, m, 480 * n:480 * n + 480], ps[:, q, 0:480], ACT.Identity, scale=-1.0,
                               bias=wqbk[:, m:m + 1]).then_inc(a_a, 1)
            for n in range(2):
                act.wait_ge(t_br, n + 1)
                act.activation(brow[0:1, 480 * n:480 * n + 480], ps[0:1, 6 + n, 0:480], ACT.Identity, scale=-1.0,
                               bias=wqbk[0:1, C:C + 1]).then_inc(a_br, 1)
            turned1(0)
            turned1(1)
            def split_first(step):
                e, kind = step // 3, step % 3
                act.wait_ge(d_ready if kind == 2 else gu_ready, e + 1)
                if kind == 2:
                    high_d(slice(e, e + 1))
                else:
                    last = high_gu(slice(e, e + 1), slice(e % RAW, e % RAW + 1), kind)
                    if kind:
                        last.then_inc(a_hg, 1)

            exps(0)
            for i in range(B):
                turned2(i)
                if i + 2 < B:
                    turned1(i + 2)
                if i:
                    act.wait_ge(v_x1, i)
                    act.dma_start(rv[i - 1], x1[:, (i - 1) % 2]).then_inc(d_row[(i - 1) % 2], 16)
                    turned3(i - 1)
                if i + 1 < B:
                    exps(i + 1)
                    split_first(i)
            act.wait_ge(v_x1, B)
            act.dma_start(rv[B - 1], x1[:, (B - 1) % 2]).then_inc(d_row[(B - 1) % 2], 16)
            act.dma_start(rows[N:N + 1, :], x1[0:1, (B - 1) % 2, 0, :]).then_inc(d_zrow, 16)
            turned3(B - 1)
            for step in range(B - 1, 3 * SPLIT):
                split_first(step)

            def gathered(m, q):
                j = 4 * m + 3 + q
                r = (3 + q) % RING
                after(act, "act", d_gath[r], 16 * (m + (3 + q) // RING + 1))
                after(act, "act", t_tx, j - 1)
                act.activation(xh[:, (3 + q) % 2, :], seat(j), ACT.Identity,
                               scale=stat[:, 0, bass.ds(j, 1)], bias=stat[:, 1, bass.ds(j, 1)]).then_inc(a_xh, 1)

            def turned_x(m, q):
                j = 4 * m + 3 + q
                after(act, "act", t_tx, j + 1)
                after(act, "act", t_gu, 4 * (j - 1))
                act.activation(xhT[:, (3 + q) % 2, 0].rearrange("p c t -> p (c t)"), ps[:, 7, 0:H],
                               ACT.Copy).then_inc(a_xhT, 1)

            def turned_h(m, q):
                j = 4 * m + 3 + q
                after(act, "act", t_th, j + 1)
                after(act, "act", t_y, j)
                act.activation(hT[:, 0, 0:4, :].rearrange("p c t -> p (c t)"), ps[:, 4, :], ACT.Copy).then_inc(a_hT, 1)
                act.activation(hT[:, 0, 4, :], ps[:, 5, 0:P], ACT.Copy)
                act.activation(hT[0:LAST, 0, 5, :], ps[0:LAST, 5, P:2 * P], ACT.Copy).then_inc(a_hT, 1)

            def silu(m, q, half):
                j = 4 * m + 3 + q
                after(act, "act", t_gu, 4 * j + 2 * half + 1)
                after(act, "act", v_h, 2 * (j - 1) + half + 1)
                act.activation(sg[:, HALF * half:HALF * half + HALF], ps[:, 2 * half, 0:HALF],
                               ACT.Silu).then_inc(a_sg, 1)

            def silus_and_split(m, q):
                j = 4 * m + 3 + q
                now = act.value_load(turn[0:1, bass.ds(j, 1)], min_val=0, max_val=1)
                with act.If(now > 0):
                    e = act.value_load(expert[0:1, bass.ds(j - 1, 1)], min_val=0, max_val=E - 1 - SPLIT)
                    after(act, "act", gu_ready, e + SPLIT + 1)
                    slot, raw = bass.ds(e % SPLIT, 1), bass.ds((e + SPLIT) % RAW, 1)
                    silu(m, q, 0)
                    silu(m, q, 1)
                    high_gu(slot, raw, 0)
                    high_gu(slot, raw, 1).then_inc(a_hg, 1)
                    after(act, "act", d_ready, e + SPLIT + 1)
                    after(act, "act", t_y, j)
                    high_d(slot, bass.ds((e + SPLIT) % 2, 1))
                with act.Else():
                    silu(m, q, 0)
                    silu(m, q, 1)
                act.sem_inc(idle["act"], 1)

            def tile(m, q, first=False, ahead1=True, ahead2=True):
                if not first:
                    turned_h(m, q - 1)
                if first:
                    silu(m, q, 0)
                    silu(m, q, 1)
                if ahead1:
                    turned_x(m, q + 1)
                if ahead2:
                    gathered(m, q + 2)
                if first:
                    return
                if ahead1:
                    silus_and_split(m, q)
                else:
                    silu(m, q, 0)
                    silu(m, q, 1)

            act.wait_ge(v_stat, 1)
            act.wait_ge(p_exp, 1)
            gathered(-1, 1)
            turned_x(-1, 1)
            gathered(-1, 2)
            every_tile(act, "act", tile, turned_h)

        @block.tensor
        def _(pe):
            pe.wait_ge(d_wq, 32)
            for m in range(C):
                for c in range(C):
                    pe.matmul(ps[:, 4 + m, 0:H + 1], wkT[:, c, P * m:P * m + P], wqT[:, c, :],
                              start=(c == 0), stop=(c == C - 1))
            for m in range(C):
                for c in range(C):
                    pe.matmul(ps[:, 4, 300 + m:301 + m], wqT[:, c, P * m:P * m + P], wkT[:, c, H:H + 1],
                              start=(c == 0), stop=(c == C - 1))
            for c in range(C):
                last = pe.matmul(ps[0:1, 5, 300:301], wqT[:, c, H:H + 1], wkT[:, c, H:H + 1],
                                 start=(c == 0), stop=(c == C - 1))
            last.then_inc(t_mt, 1)
            pe.wait_ge(d_ctx, 16)
            pe.wait_ge(a_mt, C + 2)
            for q in range(4):
                n, m = q // 2, q % 2
                for c in range(C):
                    last = pe.matmul(ps[:, q, 0:480], MT[:, c, P * m:P * m + P], ctx_sb[:, c, 480 * n:480 * n + 480],
                                     start=(c == 0), stop=(c == C - 1))
                last.then_inc(t_a, 1)
            for n in range(2):
                for c in range(C):
                    last = pe.matmul(ps[0:1, 6 + n, 0:480], MT[:, c, H:H + 1], ctx_sb[:, c, 480 * n:480 * n + 480],
                                     start=(c == 0), stop=(c == C - 1))
                last.then_inc(t_br, 1)
            pe.wait_ge(k_pool, 13)
            pe.wait_ge(d_sm, 32)
            for c in range(C):
                last = pe.matmul(ps[:, 5, 0:E], mean_w, wrT[:, c, :], start=(c == 0), stop=(c == C - 1))
            last.then_inc(t_wr, 1)

            def turn1(i):
                pe.wait_ge(v_xn, i + 1)
                if i:
                    pe.wait_ge(a_xnT, i)
                for k in range(TB):
                    for c in range(C):
                        last = pe.transpose(ps[:, 0, S * c + P * k:S * c + P * k + P],
                                            xn[:, k, P * c:P * c + P], ident[:])
                last.then_inc(t_t1, 1)

            def context(i):
                if i:
                    pe.wait_ge(v_v, i)
                for c in range(C):
                    last = pe.matmul(ps[0:K, 6, 0:H], ctx_sb[:, c, K * i:K * i + K], wv[:, c, :],
                                     start=(c == 0), stop=(c == C - 1))
                last.then_inc(t_v, 1)

            def scores(i):
                pe.wait_ge(a_xnT, i + 1)
                if i >= 2:
                    pe.wait_ge(a_exp, i - 1)
                bank = 2 + 5 * (i % 2)
                for k in range(TB):
                    for c in range(C):
                        pe.matmul(ps[:, bank, K * k:K * k + K], xnT[:, c, P * k:P * k + P],
                                  A[:, c, K * i:K * i + K], start=(c == 0), stop=False)
                    last = pe.matmul(ps[:, bank, K * k:K * k + K], ones_row[:], brow[0:1, K * i:K * i + K],
                                     start=False, stop=True)
                last.then_inc(t_s, 1)

            def turn2(i):
                pe.wait_ge(a_exp, i + 1)
                if i:
                    pe.wait_ge(a_pT, i)
                for k in range(TB):
                    last = pe.transpose(ps[0:K, 3, P * k:P * k + P], prob[:, k, :], ident[:])
                last.then_inc(t_t2, 1)

            def values(i):
                pe.wait_ge(a_pT, i + 1)
                pe.wait_ge(v_v, i + 1)
                if i:
                    pe.wait_ge(v_x1, i)
                for k in range(TB):
                    last = pe.matmul(ps[:, 4, H * k:H * k + H], pT[:, P * k:P * k + P], V[0:K, i, :],
                                     start=True, stop=True)
                last.then_inc(t_pv, 1)

            def turn3(i):
                pe.wait_ge(v_x1, i + 1)
                if i:
                    pe.wait_ge(a_x1T, i)
                for k in range(TB):
                    for c in range(C):
                        last = pe.transpose(ps[:, 1, S * c + P * k:S * c + P * k + P],
                                            x1[:, i % 2, k, P * c:P * c + P], ident[:])
                last.then_inc(t_t3, 1)

            def logits(i):
                pe.wait_ge(a_x1T, i + 1)
                pe.wait_ge(v_wrc, 1)
                if i:
                    pe.wait_ge(v_oh, i)
                for k in range(TB):
                    for c in range(C):
                        last = pe.matmul(ps[:, 5, E * k:E * k + E], x1T[:, c, P * k:P * k + P], wrc[:, c, :],
                                         start=(c == 0), stop=(c == C - 1))
                last.then_inc(t_lg, 1)

            pe.wait_ge(a_a, 4)
            turn1(0)
            pe.wait_ge(a_br, 2)
            pe.wait_ge(d_wv, 16)
            context(0)
            scores(0)
            turn1(1)
            for i in range(B):
                turn2(i)
                if i + 1 < B:
                    scores(i + 1)
                if i + 2 < B:
                    turn1(i + 2)
                values(i)
                if i:
                    turn3(i - 1)
                if i + 1 < B:
                    context(i + 1)
                if i:
                    logits(i - 1)
            turn3(B - 1)
            logits(B - 1)

            pe.wait_ge(v_sort, 1)
            pe.matmul(ps[:, 0, 0:(NTOK + 1) * E], tri[:], oh[:].rearrange("p t e -> p (t e)"), start=True, stop=False,
                      skip_group_check=True)
            for t in range(NTOK):
                last = pe.matmul(ps[:, 0, E * (t + 1):E * (NTOK + 1)].rearrange("p (t e) -> p t e", e=E), ones_b[:],
                                 oh[:, t:t + 1, :].to_broadcast([P, NTOK - t, E]), start=False, stop=(t == NTOK - 1),
                                 skip_group_check=True)
            last.then_inc(t_rk, 1)
            pe.wait_ge(v_lo, 1)
            pe.wait_ge(p_lo, 1)
            for t in range(NTOK):
                last = pe.matmul(ps[:, 2, 0:2 * NT], ohlo[:, t, :], uv[:, t].rearrange("p a n -> p (a n)"),
                                 start=(t == 0), stop=(t == NTOK - 1))
            last.then_inc(t_tab, 1)
            for t in range(NTOK):
                if t % (NTOK // 2) == 0:
                    pe.wait_ge(v_rsel, 2 * t // NTOK + 1)
                last = pe.matmul(ps[:, 3, 0:6 * NT], ohlo[:, t, :], rsel[:, t].rearrange("p a n -> p (a n)"), start=(t == 0), stop=(t == NTOK - 1))
            last.then_inc(t_stat, 1)

            pe.wait_ge(p_exp, 1)

            def turn_x(m, q):
                j = 4 * m + 3 + q
                after(pe, "pe", a_xh, j + 1)
                after(pe, "pe", v_xhT, j)
                for c in range(C):
                    last = pe.transpose(ps[:, 7, P * c:P * c + P], xh[:, (3 + q) % 2, P * c:P * c + P], ident[:])
                last.then_inc(t_tx, 1)

            def turn_h(m, q):
                j = 4 * m + 3 + q
                after(pe, "pe", v_h, 2 * (j + 1))
                after(pe, "pe", v_hT, j)
                for c in range(CI):
                    rows_ = P if c < CI - 1 else LAST
                    last = pe.transpose(ps[0:rows_, 4 + c // 4, P * (c % 4):P * (c % 4) + P],
                                        hm[:, P * c:P * c + rows_], ident[:])
                last.then_inc(t_th, 1)

            PASSES = [(0, 0), (0, 1), (1, 0)]

            def up(m, q):
                j = 4 * m + 3 + q
                e = pe.value_load(expert[0:1, bass.ds(j, 1)], min_val=0, max_val=E - 1)
                after(pe, "pe", p_lg, e + 1)
                after(pe, "pe", v_xhT, j + 1)
                slot = bass.ds(e % SPLIT, 1)
                for g in range(4):
                    for c in range(C):
                        for x_part, w_part in PASSES:
                            last = pe.matmul(ps[:, g, 0:HALF], xhT[:, (3 + q) % 2, x_part, c, :],
                                             wgu[:, slot, w_part, c, g, :].rearrange("p o n -> p (o n)"),
                                             start=(c == 0 and (x_part, w_part) == (0, 0)),
                                             stop=(c == C - 1 and (x_part, w_part) == PASSES[-1]))
                    last.then_inc(t_gu, 1)

            def down(m, q):
                j = 4 * m + 3 + q
                e = pe.value_load(expert[0:1, bass.ds(j, 1)], min_val=0, max_val=E - 1)
                after(pe, "pe", p_ld, e + 1)
                after(pe, "pe", v_hT, j + 1)
                after(pe, "pe", v_out, j)
                slot = bass.ds(e % SPLIT, 1)
                for c in range(CI):
                    rows_ = P if c < CI - 1 else LAST
                    for x_part, w_part in PASSES:
                        last = pe.matmul(ps[:, 6, 0:H], hT[0:rows_, x_part, c, :],
                                         wd[0:rows_, slot, w_part, c, :].rearrange("p o n -> p (o n)"),
                                         start=(c == 0 and (x_part, w_part) == (0, 0)),
                                         stop=(c == CI - 1 and (x_part, w_part) == PASSES[-1]))
                last.then_inc(t_y, 1)

            def tile(m, q, first=False, ahead1=True, ahead2=True):
                if not first:
                    turn_h(m, q - 1)
                if first:
                    up(m, q)
                if ahead1:
                    turn_x(m, q + 1)
                if not first:
                    up(m, q)
                    down(m, q - 1)

            def drain(m, q):
                turn_h(m, q)
                down(m, q)

            turn_x(-1, 1)
            every_tile(pe, "pe", tile, drain)

        @block.vector
        def _(dve):
            chained = [0]

            def link(ins):
                chained[0] += 1
                ins.then_inc(v_chain, 1)
                dve.wait_ge(v_chain, chained[0])

            def norm1(i):
                dve.wait_ge(v_st1, 1 if i < 2 else 2)
                if i:
                    dve.wait_ge(t_t1, i)
                for k in range(TB):
                    t = TB * i + k
                    ins = dve.tensor_scalar(xn[:, k, :], xin[:, t, :], rs1[:, t:t + 1], nm1[:, t:t + 1],
                                            ALU.mult, ALU.add)
                ins.then_inc(v_xn, 1)

            for lo, hi in ((0, 2), (2, B)):
                for b in range(lo, hi):
                    dve.wait_ge(d_x[b], 16)
                    for k in range(TB):
                        ins = dve.bn_stats(st1[:, TB * b + k, :], xin[:, TB * b + k, :])
                link(ins)
                t = slice(TB * lo, TB * hi)
                for n in range(TB * lo, TB * hi):
                    ins = dve.bn_aggr(mv1[:, n, :], st1[:, n, :])
                link(ins)
                link(guess(dve, link, mv1[:, t, 1], TB * (hi - lo)))
                newton(dve, link, mv1[:, t, 0], rs1[:, t], nm1[:, t], TB * (hi - lo)).then_inc(v_st1, 1)
                if lo == 0:
                    norm1(0)
                    dve.wait_ge(a_tg, 1)
                    link(dve.tensor_scalar(tgn[:], tg[:, 0:1], NORM, None, ALU.mult))
                    dve.wait_ge(d_sm, 32)
                    link(dve.tensor_scalar(bvt[:], bvb[:], tgn[:, 0:1], None, ALU.mult))
            dve.wait_ge(t_wr, 1)
            for c in range(C):
                ins = dve.tensor_tensor(wrc[:, c, :], wrT[:, c, :], ps[:, 5, 0:E], ALU.subtract)
            ins.then_inc(v_wrc, 1)

            def context(i):
                dve.wait_ge(t_v, i + 1)
                dve.scalar_tensor_tensor(out=V[0:K, i, :], in0=ps[0:K, 6, 0:H], scalar=tgn[0:K, 0:1], in1=bvt[0:K, :],
                                         op0=ALU.mult, op1=ALU.add).then_inc(v_v, 1)

            def minima(i):
                dve.wait_ge(t_s, i + 1)
                dve.tensor_reduce(negmax[:, TB * i:TB * i + TB], ps[:, 2 + 5 * (i % 2), 0:TB * K].rearrange("p (t k) -> p t k", k=K),
                                  AX_X, ALU.min).then_inc(v_max, 1)

            def residual(i):
                dve.wait_ge(a_exp, i + 1)
                link(dve.reciprocal(rsum[:, TB * i:TB * i + TB], ssum[:, TB * i:TB * i + TB]))
                dve.wait_ge(t_pv, i + 1)
                if i >= 2:
                    dve.wait_ge(d_row[i % 2], 16 * (i // 2))
                    dve.wait_ge(t_t3, i - 1)
                for k in range(TB):
                    t = TB * i + k
                    ins = dve.scalar_tensor_tensor(out=x1[:, i % 2, k, :], in0=ps[:, 4, H * k:H * k + H],
                                                   scalar=rsum[:, t:t + 1], in1=xin[:, t, :],
                                                   op0=ALU.mult, op1=ALU.add)
                ins.then_inc(v_x1, 1)

            def statistics(i):
                dve.wait_ge(v_x1, i + 1)
                for k in range(TB):
                    ins = dve.bn_stats(st2[:, TB * i + k, :], x1[:, i % 2, k, :])
                link(ins)
                for k in range(TB):
                    ins = dve.bn_aggr(mv2[:, TB * i + k, :], st2[:, TB * i + k, :])
                ins.then_inc(v_aggr, 1)

            def route(i):
                dve.wait_ge(t_lg, i + 1)
                for k in range(TB):
                    ins = dve.max(top8[:, TB * i + k, :], ps[:, 5, E * k:E * k + E])
                link(ins)
                for k in range(TB):
                    ins = dve.max_index(idx8[:, TB * i + k, :], top8[:, TB * i + k, :], ps[:, 5, E * k:E * k + E])
                ins.then_inc(v_oh, 1)

            dve.wait_ge(k_pool, 13)
            dve.memset(oh[:, NTOK, :], 0.0)
            norm1(1)
            context(0)
            minima(0)
            norm1(2)
            for i in range(B + 1):
                if i:
                    residual(i - 1)
                if i >= 2:
                    route(i - 2)
                if i + 1 < B:
                    minima(i + 1)
                if i + 3 < B:
                    norm1(i + 3)
                if i:
                    statistics(i - 1)
                if i + 1 < B:
                    context(i + 1)
            dve.wait_ge(v_aggr, B)
            guess(dve, link, mv2[:, :, 1], NTOK).then_inc(v_guess, 1)
            route(B - 1)
            dve.wait_ge(v_oh, B)
            link(dve.tensor_copy(pick[:], idx8[:, :, 0]))
            dve.tensor_tensor(oh[:, 0:NTOK, :], iota_e[:].to_broadcast([P, NTOK, E]), pick[:].unsqueeze(2).to_broadcast([P, NTOK, E]),
                              ALU.is_equal).then_inc(v_sort, 1)

            dve.wait_ge(v_sort, 1)
            dve.wait_ge(t_rk, 1)
            n_of, padded, ends, offs = cnt[:, 0, :], cnt[:, 1, :], cnt[:, 2, :], cnt[:, 3, :]
            link(dve.tensor_scalar(n_of, ps[:, 0, NTOK * E:(NTOK + 1) * E], 1.0, float(P - 1), ALU.max, ALU.add))
            link(dve.tensor_copy(cnt_i[:, 0, :], n_of))
            link(dve.tensor_scalar(cnt_i[:, 1, :], cnt_i[:, 0, :], 7, 7, ALU.logical_shift_right, ALU.logical_shift_left))
            link(dve.tensor_copy(padded, cnt_i[:, 1, :]))
            link(dve.memset(cnt[:, 4, :], 0.0))
            link(dve.tensor_tensor_scan(ends, padded, cnt[:, 4, :], 0.0, ALU.add, ALU.add))
            link(dve.tensor_tensor(offs, ends, padded, ALU.subtract))
            dve.tensor_tensor(past[:], starts[:].to_broadcast([P, NT, E]), cnt[:, 2:3, :].to_broadcast([P, NT, E]), ALU.is_ge)
            link(dve.tensor_tensor(rk[:], ps[:, 0, 0:NTOK * E].rearrange("p (t e) -> p t e", e=E),
                                   cnt[:, 3:4, :].to_broadcast([P, NTOK, E]), ALU.add))
            link(dve.tensor_tensor(rk[:], rk[:], oh[:, 0:NTOK, :], ALU.mult))
            link(dve.tensor_reduce(slot[:], rk[:], AX_X, ALU.add))
            link(dve.tensor_copy(slot_i[:, 0, :], slot[:]))
            dve.tensor_scalar(slot_i[:, 1, :], slot_i[:, 0, :], P - 1, None, ALU.bitwise_and)
            link(dve.tensor_scalar(slot_i[:, 2, :], slot_i[:, 0, :], 7, None, ALU.logical_shift_right))
            link(dve.tensor_copy(slot_f[:], slot_i[:, 1:3, :]))
            dve.sem_inc(v_slot, 1)
            for t in range(NTOK - SHARE):
                dve.tensor_scalar(ohlo[:, t, :], iota_lo[:], slot_f[:, 0, t:t + 1], None, ALU.is_equal)
            link(dve.tensor_tensor(ohhi[:], iota_hi[:].to_broadcast([P, NTOK, NT]), slot_f[:, 1, :].unsqueeze(2).to_broadcast([P, NTOK, NT]), ALU.is_equal))
            dve.tensor_tensor(uv[:, :, 0, :], ohhi[:], iota_t[:].to_broadcast([P, NTOK, NT]), ALU.mult)
            dve.tensor_scalar(uv[:, :, 1, :], ohhi[:], iota_p[:, 0:1], None, ALU.mult).then_inc(v_lo, 1)

            def weighed(half):
                t = slice(NTOK // 2 * half, NTOK // 2 * (half + 1))
                dims = [P, NTOK // 2, 6, NT]
                dve.tensor_tensor(rsel[:, t], ohhi[:, t].unsqueeze(2).to_broadcast(dims),
                                  r3[:, t].rearrange("p t a b -> p t (a b)").unsqueeze(3).to_broadcast(dims),
                                  ALU.mult).then_inc(v_rsel, 1)

            dve.wait_ge(p_r3, 1)
            weighed(0)
            dve.wait_ge(t_tab, 1)
            link(dve.tensor_scalar(tabf[:], ps[:, 2, 0:NT], float(P), float(N), ALU.mult, ALU.add))
            link(dve.tensor_tensor(tab2[:], tabf[:], ps[:, 2, NT:2 * NT], ALU.add))
            dve.tensor_copy(table[:], tab2[:]).then_inc(v_tab, 1)
            weighed(1)
            dve.wait_ge(t_stat, 1)
            flat = stat[:].rearrange("p a n -> p (a n)")
            link(dve.tensor_copy(flat, ps[:, 3, 4 * NT:6 * NT]))
            link(dve.tensor_tensor(flat, ps[:, 3, 2 * NT:4 * NT], flat, ALU.add))
            dve.tensor_tensor(flat, ps[:, 3, 0:2 * NT], flat, ALU.add).then_inc(v_stat, 1)

            def turned_x(m, q):
                j = 4 * m + 3 + q
                after(dve, "dve", a_xhT, j + 1)
                par = (3 + q) % 2
                dve.tensor_tensor(xhT[:, par, 1].rearrange("p c t -> p (c t)"), ps[:, 7, 0:H],
                                  xhT[:, par, 0].rearrange("p c t -> p (c t)").bitcast(F32), ALU.subtract).then_inc(v_xhT, 1)

            def turned_h(m, q):
                j = 4 * m + 3 + q
                after(dve, "dve", a_hT, 2 * j + 1)
                dve.tensor_tensor(hT[:, 1, 0:4, :].rearrange("p c t -> p (c t)"), ps[:, 4, :],
                                  hT[:, 0, 0:4, :].rearrange("p c t -> p (c t)").bitcast(F32), ALU.subtract)
                after(dve, "dve", a_hT, 2 * j + 2)
                dve.tensor_tensor(hT[:, 1, 4, :], ps[:, 5, 0:P], hT[:, 0, 4, :].bitcast(F32), ALU.subtract)
                dve.tensor_tensor(hT[0:LAST, 1, 5, :], ps[0:LAST, 5, P:2 * P], hT[0:LAST, 0, 5, :].bitcast(F32),
                                  ALU.subtract).then_inc(v_hT, 1)

            def gated(m, q):
                j = 4 * m + 3 + q
                for half in range(2):
                    after(dve, "dve", a_sg, 2 * j + half + 1)
                    after(dve, "dve", t_gu, 4 * j + 2 * half + 2)
                    after(dve, "dve", t_th, j)
                    n = slice(HALF * half, HALF * half + HALF)
                    dve.tensor_tensor(hm[:, n], sg[:, n], ps[:, 2 * half + 1, 0:HALF], ALU.mult).then_inc(v_h, 1)

            def finish(m, q):
                j = 4 * m + 3 + q
                r = (3 + q) % RING
                after(dve, "dve", t_y, j + 1)
                after(dve, "dve", d_scat[r], 16 * (m + (3 + q) // RING))
                dve.scalar_tensor_tensor(out=og[:, r, :], in0=ps[:, 6, 0:H], scalar=tg[:, 1:2], in1=seat(j),
                                         op0=ALU.mult, op1=ALU.add).then_inc(v_out, 1)

            def tile(m, q, first=False, ahead1=True, ahead2=True):
                if not first:
                    turned_h(m, q - 1)
                if first:
                    gated(m, q)
                if ahead1:
                    turned_x(m, q + 1)
                if not first:
                    gated(m, q)
                    finish(m, q - 1)

            def drain(m, q):
                turned_h(m, q)
                finish(m, q)

            dve.wait_ge(p_exp, 1)
            turned_x(-1, 1)
            every_tile(dve, "dve", tile, drain)


def kernel(x, ctx_1024, g_xattn, g_ffn, L0_xattn_Wq, L0_xattn_bq, L0_xattn_Wk, L0_xattn_bk, L0_xattn_Wv,
           L0_xattn_bv, L0_ffn_router_w, L0_ffn_gate_w, L0_ffn_up_w, L0_ffn_down_w):
    import numpy as np
    import concourse.bacc as bacc
    from concourse.bass_utils import run_bass_kernel_spmd

    def arr(a):
        return np.ascontiguousarray(a)

    gate, up, down = (np.asarray(a) for a in (L0_ffn_gate_w, L0_ffn_up_w, L0_ffn_down_w))
    gu = np.stack([gate.reshape(E, 2, HALF, C, P), up.reshape(E, 2, HALF, C, P)], axis=2)
    gu = gu.transpose(0, 5, 4, 1, 2, 3).reshape(E, P, C * 4 * HALF)
    dT = down.transpose(0, 2, 1)
    cut = (CI - 1) * P
    arrays = {
        "x": x, "ctxT": np.asarray(ctx_1024).reshape(B * K, H).T,
        "g_x": np.asarray(g_xattn).reshape(1, 1), "g_f": np.asarray(g_ffn).reshape(1, 1),
        "WqT": np.concatenate([np.asarray(L0_xattn_Wq).T, np.asarray(L0_xattn_bq).reshape(H, 1)], axis=1),
        "WkT": np.concatenate([np.asarray(L0_xattn_Wk).T, np.asarray(L0_xattn_bk).reshape(H, 1)], axis=1),
        "Wv": L0_xattn_Wv, "bv": np.asarray(L0_xattn_bv).reshape(1, H),
        "WrT": np.asarray(L0_ffn_router_w).T, "Wgu": gu,
        "Wd": dT[:, :cut].reshape(E, CI - 1, P, H).transpose(0, 2, 1, 3).reshape(E, P, (CI - 1) * H),
        "WdL": dT[:, cut:],
    }
    arrays = {f"in_{k}": arr(a) for k, a in arrays.items()}
    nc = bacc.Bacc("TRN2", target_bir_lowering=False, num_devices=1)
    args = [nc.dram_tensor(k, a.shape, mybir.dt.from_np(a.dtype), kind="ExternalInput").ap() for k, a in arrays.items()]
    out = nc.dram_tensor("out", (N, H), F32, kind="ExternalOutput").ap()
    flamingo_moe(nc, *args, out)
    r = run_bass_kernel_spmd(nc, [arrays], core_ids=[0])
    return r.results[0]["out"].reshape(B, S, H)
```
